# Optimizing a Trainium2 kernel written in Bass

```python
import numpy as np
import jax
import jax.numpy as jnp

def _softmax(x, axis=-1):
    return jax.nn.softmax(x, axis=axis)

def _gelu(x):
    return jax.nn.gelu(x, approximate=True)

def _silu(x):
    return jax.nn.silu(x)

def _sigmoid(x):
    return jax.nn.sigmoid(x)

def _layernorm(x, axis=-1, eps=1e-05):
    m = jnp.mean(x, axis=axis, keepdims=True)
    v = jnp.var(x, axis=axis, keepdims=True)
    return (x - m) / jnp.sqrt(v + eps)

def _scatter_add(tgt, idx, src, axis=0):
    return tgt.at[idx].add(src)

def _segment_sum(src, seg, n):
    return jax.ops.segment_sum(src, seg, n)
kernel_name = 'mk_flamingo_gated_d1_seqx_r8_fd175f'

def setup_inputs(seed: int=0):
    np.random.seed(seed)
    _w = jnp.asarray

    def _rec_inputs():
        import jax
        import jax.numpy as jnp
        _rk = jax.random.key(seed)
        x = 7.22e-05 + 1 * jax.random.normal(jax.random.fold_in(_rk, 1), (8, 128, 256), jnp.float32)
        _lenS = 128 - jax.random.randint(jax.random.fold_in(_rk, 7), (8,), 0, max(1, 128 // 4) + 1, jnp.int32)
        _lenS2 = 128 - jax.random.randint(jax.random.fold_in(_rk, 8), (8,), 0, max(1, 128 // 4) + 1, jnp.int32)
        _ctx_2048P = jax.random.normal(jax.random.fold_in(_rk, 11), (8, 16, 256), jnp.float32)
        _ctx_2048c = jax.random.dirichlet(jax.random.fold_in(_rk, 511), 0.3 * jnp.ones((16,), jnp.float32), (8, 128))
        _ctx_2048t = jnp.einsum('bsk,bkd->bsd', _ctx_2048c, _ctx_2048P)
        _ctx_2048t = _ctx_2048t * jax.lax.rsqrt(jnp.mean(jnp.square(_ctx_2048t)) + 1e-12) * 0.953939
        ctx_2048 = 4.13588e-05 + 0.999923 * (_ctx_2048t + 0.3 * jax.random.normal(jax.random.fold_in(_rk, 611), (8, 128, 256), jnp.float32))
        _validS = jnp.arange(128)[None, :] < _lenS[:, None]
        _validS2 = jnp.arange(128)[None, :] < _lenS2[:, None]
        _causal = jnp.tril(jnp.ones((128, 128), dtype=bool))
        mask_SxS2_bc0 = jnp.logical_not(jnp.broadcast_to(_validS2[0:1, :], (128, 128)))
        mask_BxS2_bk0 = jnp.logical_not(jnp.broadcast_to(_validS2[:, :], (8, 128)))
        _g = jax.random.normal(jax.random.fold_in(_rk, 9001), (2, 1), jnp.float32)
        _g = jnp.sign(_g) * jnp.maximum(jnp.abs(_g), 1.0) + (_g == 0) * 1.0
        g_xattn = _g[0]
        g_ffn = _g[1]
        return (x, ctx_2048, mask_SxS2_bc0, mask_BxS2_bk0, g_xattn, g_ffn)
    x, ctx_2048, mask_SxS2_bc0, mask_BxS2_bk0, g_xattn, g_ffn = _rec_inputs()

    def _L0_xattn_setup():
        import jax, jax.numpy as jnp
        import numpy as np
        B, LQ, LKV = (4, 128, 128)
        HID, H, G = (256, 32, 8)
        HD = HID // H
        HPG = H // G
        key = jax.random.key(seed)
        ks = jax.random.split(key, 10)
        s = 0.02
        inp = {'X': jax.random.normal(ks[0], (B, LQ, HID), jnp.float32), 'encoder_output': jax.random.normal(ks[1], (B, LKV, HID), jnp.float32), 'causal_mask': jnp.triu(jnp.ones((LQ, LKV), bool), 1), 'padding_mask': jnp.zeros((B, LKV), bool).at[B // 2:, LKV - LKV // 4:].set(True), 'Wq': jax.random.normal(ks[2], (HID, HID), jnp.float32) * s, 'bq': jnp.zeros((HID,), jnp.float32), 'Wk': jax.random.normal(ks[3], (G * HD, HID), jnp.float32) * s, 'bk': jnp.zeros((G * HD,), jnp.float32), 'Wv': jax.random.normal(ks[4], (G * HD, HID), jnp.float32) * s, 'bv': jnp.zeros((G * HD,), jnp.float32), 'Wo': jax.random.normal(ks[5], (HID, HID), jnp.float32) * s, 'bo': jnp.zeros((HID,), jnp.float32)}
        return inp
    _L0_xattn_all = _L0_xattn_setup()
    _L0_xattn_in = {k: v for k, v in _L0_xattn_all.items() if k in ('Wq', 'bq', 'Wk', 'bk', 'Wv', 'bv', 'Wo', 'bo')}
    del _L0_xattn_all

    def _L0_ffn_setup():
        import jax, jax.numpy as jnp
        import numpy as np
        B, T, D, F, E, K = (2, 128, 256, 96, 16, 2)
        key = jax.random.key(seed)
        k0, k1, k2, k3, k4 = jax.random.split(key, 5)
        scale = 0.02
        return {'x': jax.random.normal(k0, (B, T, D), dtype=jnp.float32), 'router_w': jax.random.normal(k1, (D, E), dtype=jnp.float32) * scale, 'gate_w': jax.random.normal(k2, (E, D, F), dtype=jnp.float32) * scale, 'up_w': jax.random.normal(k3, (E, D, F), dtype=jnp.float32) * scale, 'down_w': jax.random.normal(k4, (E, F, D), dtype=jnp.float32) * scale}
    _L0_ffn_all = _L0_ffn_setup()
    _L0_ffn_in = {k: v for k, v in _L0_ffn_all.items() if k in ('router_w', 'gate_w', 'up_w', 'down_w')}
    del _L0_ffn_all
    return {'x': x, 'ctx_2048': ctx_2048, 'mask_SxS2_bc0': mask_SxS2_bc0, 'mask_BxS2_bk0': mask_BxS2_bk0, 'g_xattn': g_xattn, 'g_ffn': g_ffn, 'L0_xattn_Wq': _L0_xattn_in['Wq'], 'L0_xattn_bq': _L0_xattn_in['bq'], 'L0_xattn_Wk': _L0_xattn_in['Wk'], 'L0_xattn_bk': _L0_xattn_in['bk'], 'L0_xattn_Wv': _L0_xattn_in['Wv'], 'L0_xattn_bv': _L0_xattn_in['bv'], 'L0_xattn_Wo': _L0_xattn_in['Wo'], 'L0_xattn_bo': _L0_xattn_in['bo'], 'L0_ffn_router_w': _L0_ffn_in['router_w'], 'L0_ffn_gate_w': _L0_ffn_in['gate_w'], 'L0_ffn_up_w': _L0_ffn_in['up_w'], 'L0_ffn_down_w': _L0_ffn_in['down_w']}

def reference(x, ctx_2048, mask_SxS2_bc0, mask_BxS2_bk0, g_xattn, g_ffn, L0_xattn_Wq, L0_xattn_bq, L0_xattn_Wk, L0_xattn_bk, L0_xattn_Wv, L0_xattn_bv, L0_xattn_Wo, L0_xattn_bo, L0_ffn_router_w, L0_ffn_gate_w, L0_ffn_up_w, L0_ffn_down_w):
    import jax
    import jax.numpy as jnp

    def _L0_xattn_ref(X, encoder_output, causal_mask, padding_mask, Wq, bq, Wk, bk, Wv, bv, Wo, bo):
        import jax, jax.numpy as jnp
        import numpy as np
        B, LQ, LKV = (4, 128, 128)
        HID, H, G = (256, 32, 8)
        HD = HID // H
        HPG = H // G
        b = X.shape[0]
        q = X @ Wq.T + bq
        k = encoder_output @ Wk.T + bk
        v = encoder_output @ Wv.T + bv
        q = q.reshape(b, LQ, G, HPG, HD).transpose(0, 2, 3, 1, 4)
        k = k.reshape(b, LKV, G, HD).transpose(0, 2, 1, 3)
        v = v.reshape(b, LKV, G, HD).transpose(0, 2, 1, 3)
        scores = jnp.einsum('bgrqd,bgkd->bgrqk', q, k) / jnp.sqrt(jnp.float32(HD))
        scores = jnp.where(causal_mask[None, None, None, :, :], -jnp.inf, scores)
        scores = jnp.where(padding_mask[:, None, None, None, :], -jnp.inf, scores)
        w = jax.nn.softmax(scores, axis=-1)
        out = jnp.einsum('bgrqk,bgkd->bgrqd', w, v)
        out = out.reshape(b, H, LQ, HD).transpose(0, 2, 1, 3).reshape(b, LQ, HID)
        return out @ Wo.T + bo

    def _L0_ffn_ref(x, router_w, gate_w, up_w, down_w):
        import jax, jax.numpy as jnp
        import numpy as np
        B, T, D, F, E, K = (2, 128, 256, 96, 16, 2)
        scores = jnp.einsum('btd,de->bte', x, router_w).astype(jnp.float32)
        probs = jax.nn.softmax(scores, axis=-1)
        routing_weights, routing_idx = jax.lax.top_k(probs, K)
        routing_weights = routing_weights / jnp.sum(routing_weights, axis=-1, keepdims=True)
        routing_weights = routing_weights.astype(x.dtype)
        one_hot = jax.nn.one_hot(routing_idx, E, dtype=x.dtype)
        combine = jnp.einsum('btk,btke->bte', routing_weights, one_hot)
        g = jnp.einsum('btd,edf->ebtf', x, gate_w)
        u = jnp.einsum('btd,edf->ebtf', x, up_w)
        h = jax.nn.silu(g) * u
        expert_out = jnp.einsum('ebtf,efd->ebtd', h, down_w)
        out = jnp.einsum('ebtd,bte->btd', expert_out, combine)
        return out
    x = x + jnp.tanh(g_xattn[0]) * _L0_xattn_ref(_layernorm(x, axis=-1), ctx_2048, mask_SxS2_bc0, mask_BxS2_bk0, L0_xattn_Wq, L0_xattn_bq, L0_xattn_Wk, L0_xattn_bk, L0_xattn_Wv, L0_xattn_bv, L0_xattn_Wo, L0_xattn_bo)
    x = x + jnp.tanh(g_ffn[0]) * _L0_ffn_ref(_layernorm(x, axis=-1), L0_ffn_router_w, L0_ffn_gate_w, L0_ffn_up_w, L0_ffn_down_w)
    return x

_drawn_inputs = setup_inputs


def setup_inputs(seed=0):
    import zlib

    import numpy as np

    out = dict(_drawn_inputs(seed))
    spreads = {'L0_xattn_bq': (0.0, 0.8),
     'L0_xattn_bk': (0.0, 0.8),
     'L0_xattn_bv': (0.0, 0.296),
     'L0_xattn_bo': (0.0, 0.1)}
    factors = {'L0_xattn_Wq': 8.0,
     'L0_xattn_Wk': 8.0,
     'L0_ffn_router_w': 8.0,
     'L0_ffn_gate_w': 8.0,
     'L0_ffn_up_w': 8.0,
     'L0_ffn_down_w': 8.0}
    for name, (base, spread) in spreads.items():
        noise = np.random.default_rng([zlib.crc32(name.encode()), seed]).standard_normal(out[name].shape)
        drawn = base * np.exp(spread * noise) if base else spread * noise
        out[name] = jnp.asarray(drawn.astype(out[name].dtype))
    for name, factor in factors.items():
        out[name] = (out[name] * factor).astype(out[name].dtype)
    return out
```

```python
import numpy as np
from contextlib import ExitStack

import concourse.bass as bass
from concourse import mybir

P = 128
NB = 8
L = 128
NT = NB * L
D = 256
DC = D // P
HD = 8
G = 8
R = 4
NQ = 2
TH = NT // NQ
TPH = NB // NQ
E = 16
F = 96
EPS = 1e-5
BIG = float(2 ** 100)
SCALE = 1.0 / float(np.sqrt(np.float32(HD)))
VW = 32
KZ = 3
WR = 3
GU = 2 * DC * F

C_ID, C_GH, C_GL, C_IOTA, C_EPS, C_MH, C_ONE, C_N = 0, 128, 136, 144, 160, 168, 176, 180

F32 = mybir.dt.float32
F32R = mybir.dt.float32r
BF16 = mybir.dt.bfloat16
U8 = mybir.dt.uint8
U32 = mybir.dt.uint32
ALU = mybir.AluOpType
ACT = mybir.ActivationFunctionType
X = mybir.AxisListType.X


def shape_constants():
    c = np.zeros((P, C_N), np.float32)
    p = np.arange(P)[:, None]
    g = np.arange(G)[None, :]
    c[:, C_ID:C_ID + P] = np.eye(P)
    c[:, C_GH:C_GH + G] = (p % 64) // HD == g
    low = (p // HD == g) & (p < 64)
    pick = ((p - 64) % G == g) & (p >= 64) & (p < 64 + 2 * G)
    c[:, C_GL:C_GL + G] = low | pick
    c[:, C_IOTA:C_IOTA + E] = np.arange(E)
    c[:, C_EPS:C_EPS + NB] = EPS
    c[:, C_MH:C_MH + NB] = -0.5
    c[:, C_ONE] = 1.0
    return c


def build(nc, x, ctx_in, m_qk, m_pad, g_x, g_f, Wq, bq, Wk, bk, Wv, bv, Wo, bo, Rw, Gw, Uw, Dw, consts, out):
    es = ExitStack()
    with es:
        def sb(name, shape, dt=F32):
            return es.enter_context(nc.sbuf_tensor(name, shape, dt))

        def sem(name):
            return es.enter_context(nc.semaphore(name))

        cst = sb("cst", [P, C_N])
        ident = cst[:, C_ID:C_ID + P]
        ident_b = sb("ident_b", [P, P], BF16)
        x_sb = sb("x_sb", [P, NB, D])
        xb_sb = sb("xb_sb", [P, NB, D])
        c_sb = sb("c_sb", [P, NB, D])
        xn = sb("xn", [P, NB, D])
        wq_n = sb("wq_n", [P, DC, D])
        wkv_n = sb("wkv_n", [P, D])
        wo_n = sb("wo_n", [P, DC, D])
        wq = [sb(f"wq{i}", [P, DC, R, 2, G, HD], F32R) for i in range(2)]
        wkv = [sb(f"wkv{i}", [P, DC, 192], F32R) for i in range(2)]
        wo = [sb(f"wo{i}", [P, DC, D], F32R) for i in range(2)]
        rw_n = sb("rw_n", [P, DC, E])
        rw = [sb(f"rw{i}", [P, DC, P], F32R) for i in range(2)]
        xT = [sb(f"xT{i}", [P, DC, NT], F32R) for i in range(2)]
        cT = [sb(f"cT{i}", [P, DC, NT], F32R) for i in range(2)]
        brow = sb("brow", [1, 384])
        bperm = sb("bperm", [1, 6 * P])
        bias = sb("bias", [P, 8])
        q1 = sb("q1", [P, R, NT], F32R)
        q2 = sb("q2", [P, R, NT], F32R)
        kh = sb("kh", [P, NT], F32R)
        kl = sb("kl", [P, NT], F32R)
        kzh = sb("kzh", [P, KZ, G, L], F32R)
        kzl = sb("kzl", [P, KZ, G, L], F32R)
        vT = sb("vT", [P, NT])
        vz = sb("vz", [P, NB, G, VW])
        mqk_u = sb("mqk_u", [P, L], U8)
        pad_u = sb("pad_u", [P, NB * L], U8)
        mqk = sb("mqk", [P, L])
        padf = sb("padf", [P, NB * L])
        cmask = sb("cmask", [P, NB, L], BF16)
        bo_b = sb("bo_b", [P, D])
        gate = sb("gate", [P, 2])
        tg = sb("tg", [P, 2])
        stats = sb("stats", [P, NB, 6])
        mv = sb("mv", [P, NB, 2])
        vare = sb("vare", [P, NB])
        rstd = sb("rstd", [P, NB])
        mneg = sb("mneg", [P, R, G])
        mt = sb("mt", [P, R, 80], F32R)
        pT = sb("pT", [P, 2, G // 2, R * L])
        o_sb = sb("o_sb", [P, 2, R * L])
        rden = sb("rden", [P, 2, R, G // 2])
        an = sb("an", [P, G, R, HD])
        aT = [sb(f"aT{i}", [P, DC, L], F32R) for i in range(2)]
        s16 = vT
        sn = sb("sn", [P, NB, E])
        top = sb("top", [P, NB, 8])
        topi = sb("topi", [P, NB, 8], U32)
        topf = sb("topf", [P, NB, 8])
        dif = sb("dif", [P, NB])
        e2 = sb("e2", [P, NB])
        den2 = sb("den2", [P, NB])
        w1 = sb("w1", [P, NB])
        w2 = sb("w2", [P, NB])
        cb1 = sb("cb1", [P, NB, E])
        cb2 = sb("cb2", [P, NB, E])
        comb = sb("comb", [P, NB, E])
        p_flat = pT[:].rearrange("p h j n -> p (h j n)")
        q_flat = q1[:].rearrange("p r n -> p (r n)")
        act_g = p_flat[0:F, 0:2 * TH].rearrange("p (s n) -> p s n", s=2)
        hf_ = p_flat[0:F, 2 * TH:3 * TH]
        hh = q_flat[0:F, 0:2 * TH].rearrange("p (s n) -> p s n", s=2)
        hl = q_flat[0:F, 2 * TH:4 * TH].rearrange("p (s n) -> p s n", s=2)
        zero = sb("zero", [P, 1])
        token = sb("token", [P, 2 * 40])
        def gu_view(t):
            return t[:, 0:WR * 2 * DC * F].rearrange("p (s m c f) -> p s m c f", s=WR, m=2, c=DC)

        def d_view(t):
            return t[0:F, WR * 2 * DC * F:WR * (2 * DC * F + D)].rearrange("p (s n) -> p s n", s=WR)

        c_flat = c_sb[:].rearrange("p b d -> p (b d)")
        cT_flat = [t[:].rearrange("p c n -> p (c n)") for t in cT]
        raw_gu, raw_d = gu_view(c_flat), d_view(c_flat)
        w_gu, w_d = [gu_view(t) for t in cT_flat], [d_view(t) for t in cT_flat]

        bank = [es.enter_context(nc.psum_tensor(f"bank{i}", [P, 512], F32)) for i in range(8)]

        d_cst, d_wkv, d_wq, d_wo, d_ctx, d_x, d_b, d_bo, d_mask, d_gate, d_rw = (
            sem(n) for n in ("d_cst", "d_wkv", "d_wq", "d_wo", "d_ctx", "d_x", "d_b", "d_bo", "d_mask", "d_gate", "d_rw"))
        d_raw = [sem(f"d_raw{i}") for i in range(WR)]
        d_out = sem("d_out")
        pool_init = sem("pool_init")
        pool_step = sem("pool_step")
        mask_ok = sem("mask_ok")
        xb_ok = sem("xb_ok")
        kz_ok = sem("kz_ok")
        var_ok = sem("var_ok")
        rstd_ok = sem("rstd_ok")
        xn_ok = sem("xn_ok")
        brow_ok = sem("brow_ok")
        job_done = sem("job_done")
        job_hi = sem("job_hi")
        job_lo = sem("job_lo")
        s_done = sem("s_done")
        max_ok = sem("max_ok")
        m_parts = sem("m_parts")
        e_rows = sem("e_rows")
        st_done = sem("st_done")
        p_done = sem("p_done")
        pv_done = sem("pv_done")
        o_ok = sem("o_ok")
        misc_done = sem("misc_done")
        misc_free = sem("misc_free")
        an_ok = sem("an_ok")
        aT_ok = sem("aT_ok")
        x1_ok = sem("x1_ok")
        vec = sem("vec")
        act = sem("act")
        tg_ok = sem("tg_ok")
        rw_ok = sem("rw_ok")
        dif_ok, e2_ok = sem("dif_ok"), sem("e2_ok")
        w_ok = sem("w_ok")
        g_done = sem("g_done")
        u_done = sem("u_done")
        a_ok = sem("a_ok")
        h_ok = sem("h_ok")
        y_done = sem("y_done")
        y_free = sem("y_free")

        JOBS = ["bias", "wkv", "wq", "wo", "c00", "c01", "c10", "c11", "k0", "v0", "k1", "v1", "vn"]
        for h in range(NQ):
            JOBS += [f"x{h}{c}" for c in range(DC)] + [f"q{h}{r}" for r in range(R)]
        NA = len(JOBS)
        JOBS2 = [f"y{h}{c}" for h in range(NQ) for c in range(DC)] + [f"s{h}" for h in range(NQ)] + ["sn"]
        JOBS += JOBS2
        jn = {n: i for i, n in enumerate(JOBS)}

        def jbank(n):
            return bank[jn[n] % 8]

        def mi(kind, b):
            if kind == "MT":
                return 0 if b == 0 else 5 * (b - 1) + 2
            if b == NB - 1:
                return 5 * b + {"TO0": 1, "TO1": 2, "AT": 3, "WO": 4}[kind]
            return 5 * b + {"TO0": 1, "TO1": 3, "AT": 4, "WO": 5}[kind]

        def mbank(kind, b):
            return bank[6 + mi(kind, b) % 2]

        def toks(t):
            return slice(t * L, (t + 1) * L)

        def half(h):
            return slice(h * TH, (h + 1) * TH)

        block = es.enter_context(nc.Block())

        @block.sync
        def _(sp):
            sp.dma_start(cst[:], consts).then_inc(d_cst, 16)
            sp.dma_start(c_sb[:, 0:TPH, :], ctx_in[0:TPH].rearrange("b p d -> p b d")).then_inc(d_ctx, 16)
            sp.dma_start(wkv_n[0:64, :], Wk).then_inc(d_wkv, 16)
            sp.dma_start(wkv_n[64:128, :], Wv).then_inc(d_wkv, 16)
            sp.dma_start(x_sb[:, 0:TPH, :], x[0:TPH].rearrange("b p d -> p b d")).then_inc(d_x, 16)
            sp.dma_start(wq_n[:], Wq.rearrange("(o p) d -> p o d", p=P)).then_inc(d_wq, 16)
            sp.wait_ge(d_ctx, 16)
            sp.dma_start(c_sb[:, TPH:NB, :], ctx_in[TPH:NB].rearrange("b p d -> p b d")).then_inc(d_ctx, 16)
            sp.wait_ge(d_x, 16)
            sp.dma_start(x_sb[:, TPH:NB, :], x[TPH:NB].rearrange("b p d -> p b d")).then_inc(d_x, 16)
            sp.dma_start(wo_n[:], Wo.rearrange("(o p) d -> p o d", p=P)).then_inc(d_wo, 16)
            sp.dma_start(mqk_u[:], m_qk).then_inc(d_mask, 16)
            sp.dma_start(pad_u[:], m_pad.rearrange("(a b) k -> a (b k)", a=1).to_broadcast([P, NB * L])).then_inc(d_mask, 16)
            sp.dma_start(rw_n[:], Rw.rearrange("(c p) e -> p c e", p=P)).then_inc(d_rw, 16)
            sp.wait_ge(job_done, jn["c11"] + 1)
            for e in range(E):
                if e >= WR:
                    sp.wait_ge(w_ok, e - WR + 1)
                s = e % WR
                sp.dma_start(raw_gu[:, s, 0], Gw[e].rearrange("(c p) f -> p c f", p=P)).then_inc(d_raw[s], 16)
                sp.dma_start(raw_gu[:, s, 1], Uw[e].rearrange("(c p) f -> p c f", p=P)).then_inc(d_raw[s], 16)
                sp.dma_start(raw_d[:, s], Dw[e]).then_inc(d_raw[s], 16)
            for h in range(NQ):
                sp.wait_ge(y_free, (E - 1) * 2 * NQ + 2 * (h + 1))
                sp.dma_start(out[h * TPH:(h + 1) * TPH].rearrange("b p d -> p b d"),
                             x_sb[:, h * TPH:(h + 1) * TPH, :]).then_inc(d_out, 16)
            sp.wait_ge(d_out, 16 * NQ)

        @block.gpsimd
        def _(pool):
            n_own = [0]

            def step(ins):
                n_own[0] += 1
                ins.then_inc(pool_step, 1)
                pool.wait_ge(pool_step, n_own[0])

            pool.memset(zero[:], 0.0)
            pool.memset(bperm[:], 0.0)
            pool.memset(mt[:].bitcast(F32), 0.0)
            pool.memset(kl[:].bitcast(F32), 1.0)
            pool.memset(q2[:].bitcast(F32), 0.0)
            pool.memset(rw[0][:].bitcast(F32), 0.0)
            pool.memset(rw[1][:].bitcast(F32), 0.0)
            pool.memset(vz[:], 0.0).then_inc(pool_init, 1)
            pool.wait_ge(pool_init, 1)
            pool.memset(vz[:, :, :, HD:HD + 1], 1.0).then_inc(pool_init, 1)
            pool.wait_ge(d_cst, 16)
            pool.tensor_copy(ident_b[:], ident).then_inc(pool_init, 1)
            for h in range(NQ):
                t = slice(h * TPH, (h + 1) * TPH)
                pool.wait_ge(var_ok, h + 1)
                step(pool.tensor_tensor(vare[:, t], mv[:, t, 1], cst[:, C_EPS:C_EPS + TPH], ALU.add))
                pool.tensor_tensor(rstd[:, t], vare[:, t], cst[:, C_MH:C_MH + TPH], ALU.pow).then_inc(rstd_ok, 1)

            def separate_keys(b):
                if b >= KZ:
                    pool.wait_ge(st_done, G * (b - KZ + 1))
                s = b % KZ
                for dst, src, col, last in ((kzh, kh, C_GH, False), (kzl, kl, C_GL, True)):
                    ins = pool.tensor_tensor(
                        dst[:, s],
                        src[:, toks(b)].bitcast(F32).unsqueeze(1).to_broadcast([P, G, L]),
                        cst[:, col:col + G].unsqueeze(2).to_broadcast([P, G, L]), ALU.mult)
                    ins.then_inc(kz_ok, 1)

            pool.wait_ge(job_lo, jn["k0"] + 1)
            separate_keys(0)
            pool.wait_ge(vec, 2)
            pool.tensor_tensor(cmask[:], padf[:].rearrange("p (b k) -> p b k", b=NB),
                               mqk[:].unsqueeze(1).to_broadcast([P, NB, L]), ALU.add).then_inc(mask_ok, 1)
            separate_keys(1)
            pool.wait_ge(tg_ok, 1)
            pool.wait_ge(d_bo, 16)
            step(pool.tensor_tensor(bo_b[:], bo_b[:], tg[:, 0:1].to_broadcast([P, D]), ALU.mult))
            pool.wait_ge(d_x, 32)
            pool.tensor_tensor(xb_sb[:], x_sb[:], bo_b[:].unsqueeze(1).to_broadcast([P, NB, D]), ALU.add).then_inc(xb_ok, 1)
            pool.wait_ge(job_lo, jn["k1"] + 1)
            separate_keys(2)

            def split_expert(e):
                s = e % WR
                pool.wait_ge(d_raw[s], 48 * (e // WR + 1))
                if e == 0:
                    pool.wait_ge(job_done, jn["v1"] + 1)
                if e >= WR:
                    pool.wait_ge(y_done, 2 * NQ * (e - WR + 1))
                gu = raw_gu[:, s]
                pool.tensor_tensor(w_gu[0][:, s], gu, zero[:].unsqueeze(2).unsqueeze(3).to_broadcast([P, 2, DC, F]), ALU.add)
                step(pool.tensor_tensor(w_d[0][:, s], raw_d[:, s], zero[0:F].to_broadcast([F, D]), ALU.add))
                pool.tensor_tensor(w_gu[1][:, s], gu, w_gu[0][:, s].bitcast(F32), ALU.subtract)
                pool.tensor_tensor(w_d[1][:, s], raw_d[:, s], w_d[0][:, s].bitcast(F32), ALU.subtract).then_inc(w_ok, 1)

            for b in range(3, NB):
                separate_keys(b)
                if b - 3 < WR:
                    split_expert(b - 3)
            for h in range(NQ):
                t = slice(h * TPH, (h + 1) * TPH)
                pool.wait_ge(var_ok, NQ + h + 1)
                step(pool.tensor_tensor(vare[:, t], mv[:, t, 1], cst[:, C_EPS:C_EPS + TPH], ALU.add))
                pool.tensor_tensor(rstd[:, t], vare[:, t], cst[:, C_MH:C_MH + TPH], ALU.pow).then_inc(rstd_ok, 1)
            for e in range(WR, E):
                split_expert(e)

        @block.scalar
        def _(sc):
            n_own = [0]

            def step(ins):
                n_own[0] += 1
                ins.then_inc(act, 1)
                sc.wait_ge(act, n_own[0])

            sc.dma_start(brow[0:1, 0:256], bq.rearrange("(a n) -> a n", a=1)).then_inc(d_b, 16)
            sc.dma_start(brow[0:1, 256:320], bk.rearrange("(a n) -> a n", a=1)).then_inc(d_b, 16)
            sc.dma_start(brow[0:1, 320:384], bv.rearrange("(a n) -> a n", a=1)).then_inc(d_b, 16)
            sc.dma_start(gate[:, 0:1], g_x.rearrange("(a n) -> a n", a=1).to_broadcast([P, 1])).then_inc(d_gate, 16)
            sc.dma_start(gate[:, 1:2], g_f.rearrange("(a n) -> a n", a=1).to_broadcast([P, 1])).then_inc(d_gate, 16)
            sc.dma_start(bo_b[:], bo.rearrange("(a n) -> a n", a=1).to_broadcast([P, D])).then_inc(d_bo, 16)
            sc.wait_ge(d_cst, 16)
            sc.wait_ge(d_gate, 32)
            nc.scalar.activation(tg[:], gate[:], ACT.Tanh).then_inc(tg_ok, 1)

            def job(name):
                sc.wait_ge(job_done, jn[name] + 1)
                ps = jbank(name)
                k = name[0]
                if name == "bias" or name in ("vn", "sn"):
                    return nc.scalar.copy(token[:, 2 * jn[name]:2 * jn[name] + 1], cst[:, C_ONE:C_ONE + 1]).then_inc(job_hi, 1)
                if name == "wkv":
                    v = ps[:, 0:256].rearrange("p (c n) -> p c n", c=DC)
                    nc.scalar.copy(wkv[0][:, :, 0:64], v[:, :, 0:64])
                    return nc.scalar.copy(wkv[0][:, :, 64:192], v).then_inc(job_hi, 1)
                if name == "wq":
                    for c in range(DC):
                        src = ps[:, c * D:(c + 1) * D].rearrange("p (g r d) -> p r g d", g=G, r=R)
                        for u in range(2):
                            ins = nc.scalar.copy(wq[0][:, c, :, u], src)
                    return ins.then_inc(job_hi, 1)
                if name == "wo":
                    return nc.scalar.copy(wo[0][:], ps[:].rearrange("p (c n) -> p c n", c=DC)).then_inc(job_hi, 1)
                if k in "xcy":
                    h, c = int(name[1]), int(name[2])
                    dst = (cT if k == "c" else xT)[0]
                    return nc.scalar.copy(dst[:, c, half(h)], ps[:]).then_inc(job_hi, 1)
                if k == "k":
                    return nc.scalar.activation(kh[:, half(int(name[1]))], ps[:], ACT.Identity,
                                                bias=bias[:, 4:5]).then_inc(job_hi, 1)
                if k == "v":
                    return nc.scalar.activation(vT[64:128, half(int(name[1]))], ps[64:128, :], ACT.Identity,
                                                bias=bias[64:128, 5:6]).then_inc(job_hi, 1)
                if k == "q":
                    h, r = int(name[1]), int(name[2])
                    nc.scalar.activation(q2[0:64, r, half(h)], ps[0:64, :], ACT.Identity, bias=bias[0:64, r:r + 1])
                    return nc.scalar.activation(q1[:, r, half(h)], ps[:], ACT.Identity,
                                                bias=bias[:, r:r + 1]).then_inc(job_hi, 1)
                if k == "s":
                    return nc.scalar.copy(s16[0:E, half(int(name[1]))], ps[0:E, :]).then_inc(job_hi, 1)

            for name in JOBS[:NA]:
                if name == "k0":
                    sc.wait_ge(job_lo, jn["bias"] + 1)
                job(name)

            def copy_o(b, hf):
                sc.wait_ge(pv_done, 2 * b + hf + 1)
                if b:
                    sc.wait_ge(misc_done, mi(f"TO{hf}", b - 1) + 1)
                nc.scalar.copy(o_sb[:, hf], bank[4 + hf][:]).then_inc(o_ok, 1)

            for b in range(NB):
                for i in range(G):
                    n = G * b + i
                    sc.wait_ge(st_done, n + 1)
                    if b and i % 4 == 0:
                        sc.wait_ge(pv_done, 2 * (b - 1) + i // 4 + 1)
                    nc.scalar.activation(pT[:, i // 4, i % 4, :], bank[2 + n % 2][:], ACT.Exp,
                                         scale=SCALE).then_inc(p_done, 1)
                    if i == 6:
                        copy_o(b, 0)
                copy_o(b, 1)
            for name in JOBS[NA:]:
                job(name)
            sc.wait_ge(dif_ok, 1)
            nc.scalar.activation(e2[:], dif[:], ACT.Exp).then_inc(e2_ok, 1)
            for e in range(E):
                for h in range(NQ):
                    n = NQ * e + h
                    sc.wait_ge(g_done, n + 1)
                    if n >= 2:
                        sc.wait_ge(h_ok, n - 1)
                    nc.scalar.activation(act_g[:, n % 2], bank[n % 2][0:F, :], ACT.Silu).then_inc(a_ok, 1)

        @block.vector
        def _(ve):
            n_own = [0]

            def own(ins):
                n_own[0] += 1
                return ins.then_inc(vec, 1)

            def settle():
                ve.wait_ge(vec, n_own[0])

            def normalise(ln):
                for h in range(NQ):
                    if ln == 0:
                        ve.wait_ge(d_x, 16 * (h + 1))
                    for t in range(h * TPH, (h + 1) * TPH):
                        own(nc.vector.bn_stats(stats[:, t], x_sb[:, t]))
                    settle()
                    for t in range(h * TPH, (h + 1) * TPH):
                        ins = nc.vector.bn_aggr(mv[:, t], stats[:, t])
                    ins.then_inc(var_ok, 1)
                    if h == 0:
                        yield
                for h in range(NQ):
                    ve.wait_ge(rstd_ok, NQ * ln + h + 1)
                    for t in range(h * TPH, (h + 1) * TPH):
                        ins = nc.vector.tensor_scalar(xn[:, t], x_sb[:, t], mv[:, t, 0:1], rstd[:, t:t + 1],
                                                      ALU.subtract, ALU.mult)
                    ins.then_inc(xn_ok, 1)
                yield

            def low(dst, ps, hi, name, bias_col=None):
                if bias_col is None:
                    return nc.vector.tensor_tensor(dst, ps, hi.bitcast(F32), ALU.subtract)
                return nc.vector.scalar_tensor_tensor(dst, ps, bias_col, hi.bitcast(F32), ALU.add, ALU.subtract)

            def job(name):
                ps = jbank(name)
                k = name[0]
                ve.wait_ge(job_hi, jn[name] + 1)
                ve.wait_ge(job_done, jn[name] + 1)
                if name == "bias":
                    ins = nc.vector.tensor_copy(bias[:, 0:6], ps[:, 0:6])
                elif name == "wkv":
                    v = ps[:, 0:256].rearrange("p (c n) -> p c n", c=DC)
                    low(wkv[1][:, :, 0:64], v[:, :, 0:64], wkv[0][:, :, 0:64], name)
                    ins = low(wkv[1][:, :, 64:192], v, wkv[0][:, :, 64:192], name)
                elif name == "wq":
                    for c in range(DC):
                        src = ps[:, c * D:(c + 1) * D].rearrange("p (g r d) -> p r g d", g=G, r=R)
                        for u in range(2):
                            ins = low(wq[1][:, c, :, u], src, wq[0][:, c, :, u], name)
                elif name == "wo":
                    ins = low(wo[1][:], ps[:].rearrange("p (c n) -> p c n", c=DC), wo[0][:], name)
                elif k in "xcy":
                    h, c = int(name[1]), int(name[2])
                    t = cT if k == "c" else xT
                    ins = low(t[1][:, c, half(h)], ps[:], t[0][:, c, half(h)], name)
                elif k == "k":
                    s = half(int(name[1]))
                    if name == "k0":
                        ve.wait_ge(pool_init, 1)
                    ins = low(kl[0:64, s], ps[0:64, :], kh[0:64, s], name, bias[0:64, 4:5])
                elif name == "vn":
                    ve.wait_ge(pool_init, 2)
                    ins = nc.vector.tensor_copy(vz[:, :, :, 0:HD], ps[:].rearrange("p (b g d) -> p b g d", b=NB, g=G))
                elif k == "q":
                    h, r = int(name[1]), int(name[2])
                    ins = low(q1[64:128, r, half(h)], ps[64:128, :], q1[64:128, r, half(h)], name, bias[64:128, r:r + 1])
                elif name == "sn":
                    ins = nc.vector.tensor_copy(sn[:], ps[:, 0:NB * E].rearrange("p (b e) -> p b e", b=NB))
                elif k in "vs":
                    return nc.vector.memset(token[:, 2 * jn[name] + 1:2 * jn[name] + 2], 0.0).then_inc(job_lo, 1)
                return ins.then_inc(job_lo, 1)

            ve.wait_ge(d_b, 48)
            ve.wait_ge(pool_init, 1)
            bp = bperm[0:1, 0:R * P].rearrange("p (r u g d) -> p r u g d", r=R, u=2, g=G)
            for u in range(2):
                nc.vector.tensor_copy(bp[:, :, u], brow[0:1, 0:256].rearrange("p (g r d) -> p r g d", g=G, r=R))
            nc.vector.tensor_copy(bperm[0:1, 512:576], brow[0:1, 256:320])
            nc.vector.tensor_copy(bperm[0:1, 576:640], brow[0:1, 256:320])
            nc.vector.tensor_copy(bperm[0:1, 704:768], brow[0:1, 320:384]).then_inc(brow_ok, 1)
            ve.wait_ge(d_mask, 32)
            own(nc.vector.tensor_scalar(mqk[:], mqk_u[:], -BIG, None, ALU.mult))
            own(nc.vector.tensor_scalar(padf[:], pad_u[:], -BIG, None, ALU.mult))
            ln1 = normalise(0)
            next(ln1)
            ve.wait_ge(d_rw, 16)
            own(nc.vector.tensor_copy(rw[0][:, :, 0:E], rw_n[:]))
            settle()
            own(nc.vector.tensor_tensor(rw[1][:, :, 0:E], rw_n[:], rw[0][:, :, 0:E].bitcast(F32), ALU.subtract))
            for name in JOBS[:jn["c00"]]:
                job(name)
            next(ln1)
            for name in JOBS[jn["c00"]:NA]:
                job(name)

            def row_max(b, i):
                n = G * b + i
                r, hf = i // 2, i % 2
                ve.wait_ge(s_done, n + 1)
                nc.vector.tensor_reduce(mneg[:, r, 4 * hf:4 * hf + 4], bank[n % 2][:].rearrange("p (g k) -> p g k", g=4),
                                        X, ALU.max, negate=True).then_inc(max_ok, 1)

            def max_parts(b):
                ve.wait_ge(max_ok, G * (b + 1))
                if b:
                    ve.wait_ge(misc_done, mi("MT", b - 1) + 1)
                own(nc.vector.tensor_copy(mt[:, :, 64:72], mneg[:]))
                settle()
                nc.vector.tensor_tensor(mt[:, :, 72:80], mneg[:], mt[:, :, 64:72].bitcast(F32), ALU.subtract).then_inc(m_parts, 1)

            def take_max_rows(b):
                ve.wait_ge(misc_done, mi("MT", b) + 1)
                nc.vector.tensor_copy(q2[64:80, :, toks(b)],
                                      mbank("MT", b)[64:80, :].rearrange("p (r q) -> p r q", r=R)).then_inc(misc_free, 1)

            def norm_rows(b, hf):
                n = mi(f"TO{hf}", b)
                ve.wait_ge(misc_done, n + 1)
                v = mbank(f"TO{hf}", b)[:].rearrange("p (r j c) -> p r j c", r=R, c=VW)
                own(nc.vector.reciprocal(rden[:, hf], v[:, :, :, HD]))
                settle()
                if b and hf == 0:
                    ve.wait_ge(misc_done, mi("AT", b - 1) + 1)
                a = an[:, 4 * hf:4 * hf + 4].rearrange("p j r d -> p r j d")
                nc.vector.tensor_tensor(a, v[:, :, :, 0:HD], rden[:, hf].unsqueeze(3).to_broadcast([P, R, 4, HD]),
                                        ALU.mult).then_inc(misc_free, 1)

            def split_aT(b):
                ve.wait_ge(misc_done, mi("AT", b) + 1)
                ps = mbank("AT", b)[:, 0:D].rearrange("p (c q) -> p c q", c=DC)
                if b:
                    ve.wait_ge(misc_done, mi("WO", b - 1) + 1)
                own(nc.vector.tensor_copy(aT[0][:], ps))
                settle()
                nc.vector.tensor_tensor(aT[1][:], ps, aT[0][:].bitcast(F32), ALU.subtract).then_inc(misc_free, 1)

            def residual(b):
                ve.wait_ge(misc_done, mi("WO", b) + 1)
                if b == 0:
                    ve.wait_ge(xb_ok, 1)
                nc.vector.scalar_tensor_tensor(x_sb[:, b], mbank("WO", b)[:, 0:D], tg[:, 0:1], xb_sb[:, b],
                                               ALU.mult, ALU.add).then_inc(misc_free, 1)

            for i in range(G):
                row_max(0, i)
            max_parts(0)
            take_max_rows(0)
            for b in range(NB):
                for i in range(G):
                    if b + 1 < NB:
                        row_max(b + 1, i)
                    if b and i == 0:
                        norm_rows(b - 1, 1)
                    if b and i == 2:
                        split_aT(b - 1)
                    if b and i == 4:
                        residual(b - 1)
                if b + 1 < NB:
                    max_parts(b + 1)
                norm_rows(b, 0)
                if b + 1 < NB:
                    take_max_rows(b + 1)
            norm_rows(NB - 1, 1)
            split_aT(NB - 1)
            residual(NB - 1)

            ve.wait_ge(misc_free, 5 * NB)
            ln2 = normalise(1)
            next(ln2)
            next(ln2)
            for name in JOBS[NA:]:
                job(name)
            ve.wait_ge(job_lo, jn["sn"] + 1)
            for t in range(NB):
                own(nc.vector.max(top[:, t], sn[:, t]))
            settle()
            for t in range(NB):
                own(nc.vector.max_index(topi[:, t], top[:, t], sn[:, t]))
            nc.vector.tensor_tensor(dif[:], top[:, :, 1], top[:, :, 0], ALU.subtract).then_inc(dif_ok, 1)
            settle()
            own(nc.vector.tensor_copy(topf[:, :, 0:2], topi[:, :, 0:2]))
            ve.wait_ge(e2_ok, 1)
            own(nc.vector.tensor_scalar(den2[:], e2[:], 1.0, None, ALU.add))
            settle()
            own(nc.vector.reciprocal(w1[:], den2[:]))
            settle()
            own(nc.vector.tensor_scalar(w1[:], w1[:], tg[:, 1:2], None, ALU.mult))
            settle()
            own(nc.vector.tensor_tensor(w2[:], w1[:], e2[:], ALU.mult))
            settle()
            for t in range(NB):
                iota = cst[:, C_IOTA:C_IOTA + E]
                own(nc.vector.tensor_scalar(cb1[:, t], iota, topf[:, t, 0:1], w1[:, t:t + 1], ALU.is_equal, ALU.mult))
                own(nc.vector.tensor_scalar(cb2[:, t], iota, topf[:, t, 1:2], w2[:, t:t + 1], ALU.is_equal, ALU.mult))
            settle()
            own(nc.vector.tensor_tensor(comb[:], cb1[:], cb2[:], ALU.add))
            settle()

            def hidden(n):
                ve.wait_ge(a_ok, n + 1)
                ve.wait_ge(u_done, n + 1)
                if n:
                    ve.wait_ge(h_ok, n)
                own(nc.vector.tensor_tensor(hf_, act_g[:, n % 2], bank[2 + n % 2][0:F, :], ALU.mult))
                settle()
                if n >= 2:
                    ve.wait_ge(y_done, 2 * (n - 1))
                own(nc.vector.tensor_copy(hh[:, n % 2], hf_))
                settle()
                nc.vector.tensor_tensor(hl[:, n % 2], hf_, hh[:, n % 2].bitcast(F32), ALU.subtract).then_inc(h_ok, 1)

            def add_up(n):
                e, h = n // NQ, n % NQ
                for y in range(2):
                    m = 2 * n + y
                    ve.wait_ge(y_done, m + 1)
                    for u in range(2):
                        t = h * TPH + 2 * y + u
                        ins = nc.vector.scalar_tensor_tensor(x_sb[:, t], bank[4 + m % 4][:, u * D:(u + 1) * D],
                                                             comb[:, t, e:e + 1], x_sb[:, t], ALU.mult, ALU.add)
                    ins.then_inc(y_free, 1)

            for n in range(NQ * E + 1):
                if n < NQ * E:
                    hidden(n)
                if n >= 1:
                    if n >= 1 + NQ:
                        ve.wait_ge(y_free, 2 * (n - NQ))
                    add_up(n - 1)

        @block.tensor
        def _(pe):
            def mm(dst, a, b, start, stop):
                return nc.tensor.matmul(dst, a, b, start=start, stop=stop, skip_group_check=True)

            def three(dst, st, mv_, chunks):
                terms = [(st[0], mv_[0]), (st[0], mv_[1]), (st[1], mv_[0])]
                last = None
                for c in range(chunks):
                    for k, (a, b) in enumerate(terms):
                        last = mm(dst, a(c), b(c), c == 0 and k == 0, c == chunks - 1 and k == 2)
                return last

            def job(name):
                n = jn[name]
                if n >= 8:
                    pe.wait_ge(job_lo, n - 7)
                ps = jbank(name)
                k = name[0]
                if name == "bias":
                    pe.wait_ge(brow_ok, 1)
                    pe.wait_ge(d_cst, 16)
                    for j in range(6):
                        ins = mm(ps[:, j:j + 1], bperm[0:1, j * P:(j + 1) * P], cst[0:1, C_ONE:C_ONE + 1], True, True)
                elif name == "wkv":
                    pe.wait_ge(d_wkv, 32)
                    for c in range(DC):
                        ins = nc.tensor.transpose(ps[:, c * P:(c + 1) * P], wkv_n[:, c * P:(c + 1) * P], ident)
                elif name in ("wq", "wo"):
                    src = wq_n if name == "wq" else wo_n
                    pe.wait_ge(d_wq if name == "wq" else d_wo, 16)
                    for c in range(DC):
                        for o in range(DC):
                            ins = nc.tensor.transpose(ps[:, c * D + o * P:c * D + (o + 1) * P],
                                                      src[:, o, c * P:(c + 1) * P], ident)
                elif k in "xcy":
                    h, c = int(name[1]), int(name[2])
                    if k == "c":
                        pe.wait_ge(d_ctx, 16 * (h + 1))
                    else:
                        pe.wait_ge(xn_ok, (h + 1) + (NQ if k == "y" else 0))
                    src = c_sb if k == "c" else xn
                    for t in range(TPH):
                        ins = nc.tensor.transpose(ps[:, toks(t)], src[:, h * TPH + t, c * P:(c + 1) * P], ident)
                elif name == "vn":
                    pe.wait_ge(job_hi, jn["v1"] + 1)
                    for b in range(NB):
                        ins = nc.tensor.transpose(ps[:, b * 64:(b + 1) * 64], vT[64:128, toks(b)], ident[64:128, 64:128])
                elif k in "kv":
                    h = int(name[1])
                    pe.wait_ge(job_lo, jn[f"c{h}1"] + 1)
                    cols = slice(0, 128) if k == "k" else slice(64, 192)
                    ins = three(ps[:], [lambda c, i=i: wkv[i][:, c, cols] for i in range(2)],
                                [lambda c, i=i: cT[i][:, c, half(h)] for i in range(2)], DC)
                elif k == "q":
                    h, r = int(name[1]), int(name[2])
                    pe.wait_ge(job_lo, jn[f"x{h}1"] + 1)
                    ins = three(ps[:], [lambda c, i=i: wq[i][:, c, r].rearrange("p u g d -> p (u g d)") for i in range(2)],
                                [lambda c, i=i: xT[i][:, c, half(h)] for i in range(2)], DC)
                elif name == "sn":
                    pe.wait_ge(job_hi, jn["s1"] + 1)
                    for t in range(NB):
                        ins = nc.tensor.transpose(ps[:, t * E:(t + 1) * E], s16[0:E, toks(t)], ident[0:E, 0:E])
                elif k == "s":
                    h = int(name[1])
                    pe.wait_ge(job_lo, jn[f"y{h}1"] + 1)
                    ins = three(ps[:], [lambda c, i=i: rw[i][:, c] for i in range(2)],
                                [lambda c, i=i: xT[i][:, c, half(h)] for i in range(2)], DC)
                ins.then_inc(job_done, 1)

            for name in JOBS[:NA]:
                job(name)

            def scores_q(b, i):
                n = G * b + i
                r, hf = i // 2, i % 2
                if n >= 2:
                    pe.wait_ge(max_ok, n - 1)
                if i == 0:
                    pe.wait_ge(kz_ok, 2 * (b + 1))
                s, g4, ps = b % KZ, slice(4 * hf, 4 * hf + 4), bank[n % 2]
                mm(ps[:], q1[:, r, toks(b)], kzh[:, s, g4].rearrange("p g k -> p (g k)"), True, False)
                mm(ps[:], q2[:, r, toks(b)], kzl[:, s, g4].rearrange("p g k -> p (g k)"), False, False)
                mm(ps[:], ident_b[:], cmask[:, b].unsqueeze(1).to_broadcast([P, 4, L]), False, True).then_inc(s_done, 1)

            def scores_k(b, g):
                n = G * b + g
                if n >= 2:
                    pe.wait_ge(p_done, n - 1)
                s, ps = b % KZ, bank[2 + n % 2][:].rearrange("p (r q) -> p r q", r=R)
                mm(ps, kzh[:, s, g], q1[:, :, toks(b)], True, False)
                mm(ps, cmask[:, b], ident_b[:].unsqueeze(1).to_broadcast([P, R, L]), False, False)
                mm(ps, kzl[:, s, g], q2[:, :, toks(b)], False, True).then_inc(st_done, 1)

            def weigh_values(b, hf):
                pe.wait_ge(p_done, G * b + 4 * hf + 4)
                if b:
                    pe.wait_ge(o_ok, 2 * (b - 1) + hf + 1)
                for j in range(4):
                    ins = mm(bank[4 + hf][VW * j:VW * (j + 1), :], vz[:, b, 4 * hf + j], pT[:, hf, j], True, True)
                ins.then_inc(pv_done, 1)

            def misc(kind, b):
                n = mi(kind, b)
                if n >= 2:
                    pe.wait_ge(misc_free, n - 1)
                ps = mbank(kind, b)
                if kind == "MT":
                    pe.wait_ge(m_parts, b + 1)
                    for r in range(R):
                        ins = nc.tensor.transpose(ps[0:80, r * L:(r + 1) * L], mt[:, r].bitcast(F32), ident)
                elif kind in ("TO0", "TO1"):
                    hf = int(kind[2])
                    pe.wait_ge(o_ok, 2 * b + hf + 1)
                    for r in range(R):
                        ins = nc.tensor.transpose(ps[:, r * P:(r + 1) * P], o_sb[:, hf, r * L:(r + 1) * L], ident)
                elif kind == "AT":
                    pe.wait_ge(misc_free, mi("TO1", b) + 1)
                    a = an[:].rearrange("p g r d -> p (g r d)")
                    for c in range(DC):
                        ins = nc.tensor.transpose(ps[:, c * L:(c + 1) * L], a[:, c * P:(c + 1) * P], ident)
                elif kind == "WO":
                    pe.wait_ge(misc_free, mi("AT", b) + 1)
                    ins = three(ps[:, 0:D], [lambda c, i=i: aT[i][:, c] for i in range(2)],
                                [lambda c, i=i: wo[i][:, c] for i in range(2)], DC)
                ins.then_inc(misc_done, 1)

            pe.wait_ge(job_lo, NA)
            pe.wait_ge(mask_ok, 1)
            pe.wait_ge(pool_init, 3)
            for i in range(G):
                scores_q(0, i)
            misc("MT", 0)
            pe.wait_ge(misc_free, 1)
            for b in range(NB):
                for i in range(G):
                    if i == 0:
                        pe.wait_ge(misc_free, mi("MT", b) + 1)
                    scores_k(b, i)
                    if b + 1 < NB:
                        scores_q(b + 1, i)
                    if b and i == 0:
                        misc("TO1", b - 1)
                    if b and i == 2:
                        misc("AT", b - 1)
                    if b and i == 4:
                        misc("WO", b - 1)
                    if i == 5:
                        weigh_values(b, 0)
                misc("TO0", b)
                weigh_values(b, 1)
                if b + 1 < NB:
                    misc("MT", b + 1)
            misc("TO1", NB - 1)
            misc("AT", NB - 1)
            misc("WO", NB - 1)
            pe.wait_ge(misc_free, 5 * NB)
            for name in JOBS[NA:]:
                job(name)

            def up(n):
                e, h = n // NQ, n % NQ
                s = e % WR
                if h == 0:
                    pe.wait_ge(w_ok, e + 1)
                if n == 0:
                    pe.wait_ge(job_lo, len(JOBS))
                if n >= 2:
                    pe.wait_ge(h_ok, n - 1)
                for m, done in ((0, g_done), (1, u_done)):
                    three(bank[2 * m + n % 2][0:F, :], [lambda c, i=i: w_gu[i][:, s, m, c] for i in range(2)],
                          [lambda c, i=i: xT[i][:, c, half(h)] for i in range(2)], DC).then_inc(done, 1)

            def down(n):
                e, h = n // NQ, n % NQ
                s = e % WR
                pe.wait_ge(h_ok, n + 1)
                for y in range(2):
                    m = 2 * n + y
                    if m >= 4:
                        pe.wait_ge(y_free, m - 3)
                    for u in range(2):
                        t = 2 * y + u
                        ins = three(bank[4 + m % 4][:, u * D:(u + 1) * D],
                                    [lambda c, i=i: (hh, hl)[i][:, n % 2, toks(t)] for i in range(2)],
                                    [lambda c, i=i: w_d[i][:, s] for i in range(2)], 1)
                    ins.then_inc(y_done, 1)

            for n in range(NQ * E + 1):
                if n < NQ * E:
                    up(n)
                if n >= 1:
                    down(n - 1)


_INS = ['x', 'ctx_2048', 'mask_SxS2_bc0', 'mask_BxS2_bk0', 'g_xattn', 'g_ffn', 'L0_xattn_Wq', 'L0_xattn_bq',
        'L0_xattn_Wk', 'L0_xattn_bk', 'L0_xattn_Wv', 'L0_xattn_bv', 'L0_xattn_Wo', 'L0_xattn_bo',
        'L0_ffn_router_w', 'L0_ffn_gate_w', 'L0_ffn_up_w', 'L0_ffn_down_w']


def kernel(**inputs):
    import concourse.bacc as _bacc
    from concourse.bass_utils import run_bass_kernel_spmd as _run

    nc = _bacc.Bacc("TRN2", target_bir_lowering=False, num_devices=1)
    arrays, args = {}, []
    for name in _INS:
        a = np.ascontiguousarray(inputs[name])
        arrays[f"in_{name}"] = a
        args.append(nc.dram_tensor(f"in_{name}", a.shape, mybir.dt.from_np(a.dtype), kind="ExternalInput").ap())
    c = shape_constants()
    arrays["shape_constants"] = c
    args.append(nc.dram_tensor("shape_constants", c.shape, F32, kind="ExternalInput").ap())
    args.append(nc.dram_tensor("out_0", (NB, L, D), F32, kind="ExternalOutput").ap())
    build(nc, *args)
    r = _run(nc, [arrays], core_ids=[0])
    return r.results[0]["out_0"]
```

```python
import numpy as np
from contextlib import ExitStack

import concourse.bass as bass
from concourse import mybir

P = 128
NB = 8
L = 128
NT = NB * L
D = 256
DC = D // P
HD = 8
G = 8
R = 4
GH = G // 2
QR = GH * HD
NQ = 2
TH = NT // NQ
TPH = NB // NQ
E = 16
F = 96
EPS = 1e-5
BIG = float(2 ** 100)
SCALE = 1.0 / float(np.sqrt(np.float32(HD)))
VW = 32
KR = 3 * QR + 2 * G
KZ = 3
LEAD = 12
CH = NB * G
FT = E * F // P
WR = 2
GUC = 2 * DC * P

C_ID, C_G, C_IOTA, C_EPS, C_MH, C_ONE, C_N = 0, 128, 144, 160, 168, 176, 180

F32 = mybir.dt.float32
F32R = mybir.dt.float32r
BF16 = mybir.dt.bfloat16
U8 = mybir.dt.uint8
U32 = mybir.dt.uint32
ALU = mybir.AluOpType
ACT = mybir.ActivationFunctionType
X = mybir.AxisListType.X


def shape_constants():
    c = np.zeros((P, C_N), np.float32)
    p = np.arange(P)[:, None]
    g = np.arange(G)[None, :]
    c[:, C_ID:C_ID + P] = np.eye(P)
    score = (p % QR // HD == g % GH) & (p < 3 * QR)
    maxima = ((p - 3 * QR) % G == g) & (p >= 3 * QR) & (p < KR)
    c[:, C_G:C_G + G] = score | maxima
    c[:, C_IOTA:C_IOTA + E] = np.arange(E)
    c[:, C_EPS:C_EPS + NB] = EPS
    c[:, C_MH:C_MH + NB] = -0.5
    c[:, C_ONE] = 1.0
    return c


def expert_rows():
    e = np.arange(2 * E)[:, None] % E
    return (np.arange(FT * P)[None, :] // F == e).astype(np.bool_)


def build(nc, x, ctx_in, m_qk, m_pad, g_x, g_f, Wq, bq, Wk, bk, Wv, bv, Wo, bo, Rw, Gw, Uw, Dw, consts, pick, out):
    es = ExitStack()
    with es:
        def sb(name, shape, dt=F32):
            return es.enter_context(nc.sbuf_tensor(name, shape, dt))

        def sem(name):
            return es.enter_context(nc.semaphore(name))

        cst = sb("cst", [P, C_N])
        ident = cst[:, C_ID:C_ID + P]
        ident_b = sb("ident_b", [P, P], BF16)
        x_sb = sb("x_sb", [P, NB, D])
        xb_sb = sb("xb_sb", [P, NB, D])
        c_sb = sb("c_sb", [P, NB, D])
        xn = sb("xn", [P, NB, D])
        wq_n = sb("wq_n", [P, DC, D])
        wkv_n = sb("wkv_n", [P, D])
        wo_n = sb("wo_n", [P, DC, D])
        NQW, NKW = DC * D, DC * P
        w_t = sb("w_t", [P, FT * P + NT], F32R)
        wq = [w_t[:, i * NQW:(i + 1) * NQW].rearrange("p (c n) -> p c n", c=DC) for i in range(2)]
        wkv = [w_t[:, 2 * NQW + i * NKW:2 * NQW + (i + 1) * NKW].rearrange("p (c n) -> p c n", c=DC) for i in range(2)]
        wo = [sb(f"wo{i}", [P, DC, D], F32R) for i in range(2)]
        rw_n = sb("rw_n", [P, DC, E])
        rw = [sb(f"rw{i}", [P, DC, P], F32R) for i in range(2)]
        xT = [sb(f"xT{i}", [P, DC, NT], F32R) for i in range(2)]
        cT = [sb(f"cT{i}", [P, DC, NT], F32R) for i in range(2)]
        NBC = 2 * R + 3
        bperm = sb("bperm", [NBC, P])
        bias = sb("bias", [P, 16])
        q4 = sb("q4", [P, 2, R, NT], F32R)
        k4 = sb("k4", [P, 2, NT], F32R)
        kz = sb("kz", [P, KZ, G, L], F32R)
        vT = sb("vT", [P, NT])
        vz = sb("vz", [P, NB, G, VW])
        mqk_u = sb("mqk_u", [P, L], U8)
        pad_u = sb("pad_u", [P, NB * L], U8)
        mqk = sb("mqk", [P, L])
        padf = sb("padf", [P, NB * L])
        cmask = sb("cmask", [P, NB, L], BF16)
        bo_b = sb("bo_b", [P, D])
        gate = sb("gate", [P, 2])
        tg = sb("tg", [P, 2])
        stats = sb("stats", [P, NB, 6])
        mv = sb("mv", [P, NB, 2])
        vare = sb("vare", [P, NB])
        rstd = sb("rstd", [P, NB])
        mneg = sb("mneg", [P, R, G])
        mt = sb("mt", [P, R, KR], F32R)
        pT = sb("pT", [P, 2, G // 2, R * L])
        o_sb = sb("o_sb", [P, 2, R * L])
        rden = sb("rden", [P, 2, R, G // 2])
        an = sb("an", [P, G, R, HD])
        aT = [sb(f"aT{i}", [P, DC, L], F32R) for i in range(2)]
        s16 = vT
        sn = sb("sn", [P, NB, E])
        top = sb("top", [P, NB, 8])
        topi = sb("topi", [P, NB, 8], U32)
        topf = sb("topf", [P, NB, 8])
        dif = sb("dif", [P, NB])
        e2 = sb("e2", [P, NB])
        den2 = sb("den2", [P, NB])
        w1 = sb("w1", [P, NB])
        w2 = sb("w2", [P, NB])
        cb1 = sb("cb1", [P, NB, E])
        cb2 = sb("cb2", [P, NB, E])
        comb = sb("comb", [P, NB, E])
        p_flat = pT[:].rearrange("p h j n -> p (h j n)")
        q_flat = q4[:].rearrange("p h r n -> p (h r n)")
        act_g = p_flat[:, 0:2 * TH].rearrange("p (s n) -> p s n", s=2)
        h_su = p_flat[:, 2 * TH:3 * TH]
        h_all = p_flat[:, 3 * TH:4 * TH]
        hh = q_flat[:, 0:2 * TH].rearrange("p (s n) -> p s n", s=2)
        hl = q_flat[:, 2 * TH:4 * TH].rearrange("p (s n) -> p s n", s=2)
        c2 = sb("c2", [P, NB, 2, E], F32R)
        pick_n = sb("pick_n", [2 * E, FT * P], U8)
        pick_r = w_t[:, 0:FT * P]
        cwT = w_t[:, FT * P:FT * P + NT]
        zero = sb("zero", [P, 1])
        def gu_view(t):
            return t[:, 0:WR * GUC].rearrange("p (s m c f) -> p s m c f", s=WR, m=2, c=DC)

        def d_view(t):
            return t[:, WR * GUC:WR * (GUC + D)].rearrange("p (s n) -> p s n", s=WR)

        c_flat = c_sb[:].rearrange("p b d -> p (b d)")
        cT_flat = [t[:].rearrange("p c n -> p (c n)") for t in cT]
        raw_gu, raw_d = gu_view(c_flat), d_view(c_flat)
        w_gu, w_d = [gu_view(t) for t in cT_flat], [d_view(t) for t in cT_flat]

        bank = [es.enter_context(nc.psum_tensor(f"bank{i}", [P, 512], F32)) for i in range(8)]

        d_cst, d_wkv, d_wq, d_wo, d_ctx, d_x, d_b, d_bo, d_mask, d_gate, d_rw, d_pick = (
            sem(n) for n in ("d_cst", "d_wkv", "d_wq", "d_wo", "d_ctx", "d_x", "d_b", "d_bo", "d_mask", "d_gate",
                             "d_rw", "d_pick"))
        d_raw = [sem(f"d_raw{i}") for i in range(WR)]
        d_out = sem("d_out")
        pool_init = sem("pool_init")
        pool_step = sem("pool_step")
        mask_ok = sem("mask_ok")
        xb_ok = sem("xb_ok")
        kz_ok = sem("kz_ok")
        pick_ok = sem("pick_ok")
        var_ok = sem("var_ok")
        rstd_ok = sem("rstd_ok")
        xn_ok = sem("xn_ok")
        brow_ok = sem("brow_ok")
        d_k4 = [sem(f"d_k4_{h}") for h in range(NQ)]
        d_q4 = [[sem(f"d_q4_{h}_{r}") for r in range(R)] for h in range(NQ)]
        job_done = sem("job_done")
        job_hi = sem("job_hi")
        job_lo = sem("job_lo")
        mt_ok = sem("mt_ok")
        s_done = sem("s_done")
        max_ok = sem("max_ok")
        m_parts = sem("m_parts")
        st_done = sem("st_done")
        p_done = sem("p_done")
        pv_done = sem("pv_done")
        o_ok = sem("o_ok")
        masks_f = sem("masks_f")
        rw_ok = sem("rw_ok")
        vec = sem("vec")
        tg_ok = sem("tg_ok")
        dif_ok, e2_ok, c2_ok = sem("dif_ok"), sem("e2_ok"), sem("c2_ok")
        w_ok = sem("w_ok")
        g_done = sem("g_done")
        u_done = sem("u_done")
        u_free = sem("u_free")
        a_ok = sem("a_ok")
        h_ok = sem("h_ok")
        y_done = sem("y_done")
        fin_ok = sem("fin_ok")

        PHASE_A = [("wkv",), ("c", 0, 0), ("c", 0, 1), ("wq",), ("x", 0, 0), ("x", 0, 1), ("bias",), ("kv", 0),
                   ("q", 0, 0), ("q", 0, 1), ("MT", 0)]
        AT_SLOT = {("vn", 0): 0, ("c", 1, 0): 1, ("c", 1, 1): 2, ("x", 1, 0): 3, ("x", 1, 1): 4, ("wo",): 6,
                   ("kv", 1): 8, ("q", 1, 0): 9, ("q", 1, 1): 11, ("vn", 1): 16}
        for b in range(NB):
            if b:
                AT_SLOT["MT", b] = G * b - 3
            AT_SLOT["TO", b, 0] = G * b + 7
            AT_SLOT["TO", b, 1] = G * b + 10
            AT_SLOT["AT", b] = G * b + 12
            AT_SLOT["WO", b] = G * b + 14
            AT_SLOT["YT", b] = G * b + 19
        ROUTE = {0: 48, 1: 77}
        for h, s in ROUTE.items():
            AT_SLOT["SC", h] = s
            AT_SLOT["SN", h] = s + 1
            AT_SLOT["CT", h] = s + 8
        ORDER = [(0, 0), (1, 0), (0, 1), (1, 1)] + [(t, h) for t in range(2, FT) for h in range(NQ)]
        LASTN = {t: max(n for n, (u, _) in enumerate(ORDER) if u == t) for t in range(FT)}
        UP_SLOT = {0: 64, 1: 67, 2: 78}
        CB_SLOT = {0: 65, 1: 68}
        DOWN_SLOT = {0: 69, 1: 72}
        SLOTS = 90
        for n, s in CB_SLOT.items():
            AT_SLOT["CB", n] = s
        LATER = sorted(AT_SLOT, key=lambda j: AT_SLOT[j])
        LATER += [("CB", n) for n in range(2, len(ORDER))]
        JOBS = PHASE_A + LATER
        NA = len(PHASE_A)
        jn = {j: n for n, j in enumerate(JOBS)}
        ALL = (0, 1, 2, 3)
        hn, count = {}, 0
        for j in JOBS:
            if j[0] in ("wkv", "wq", "wo", "c", "x", "kv", "q", "AT", "YT"):
                hn[j] = count
                count += 4 if j[0] == "q" else 1
        ln = {j: n for n, j in enumerate(j for j in JOBS if j[0] != "MT")}

        def emptied(j):
            return (mt_ok, j[1] + 1) if j[0] == "MT" else (job_lo, ln[j] + 1)
        BANK = {j: 2 + n % 6 if n < NA - 1 else 6 + n % 2 for n, j in enumerate(JOBS)}

        def jbank(j):
            return bank[BANK[j]]

        def before(j):
            same = [k for k in JOBS[:jn[j]] if BANK[k] == BANK[j]]
            return same[-1] if same else None

        def jobs_at(s):
            return [j for j in LATER if AT_SLOT.get(j) == s]

        def takes_at(s):
            return ([(j, (2, 3)) for j in jobs_at(s - 2) if j[0] == "q"] +
                    [(j, (0, 1) if j[0] == "q" else ALL) for j in jobs_at(s - 1)])

        def toks(t):
            return slice(t * L, (t + 1) * L)

        def half(h):
            return slice(h * TH, (h + 1) * TH)

        def pieces(t):
            out_, at = [], P * t
            while at < P * (t + 1):
                e = at // F
                n = min((e + 1) * F, P * (t + 1)) - at
                out_.append((e, at - e * F, at - e * F + n, at - P * t))
                at += n
            return out_

        block = es.enter_context(nc.Block())

        @block.sync
        def _(sp):
            sp.dma_start(x_sb[:, 0:TPH, :], x[0:TPH].rearrange("b p d -> p b d")).then_inc(d_x, 16)
            sp.dma_start(c_sb[:, 0:TPH, :], ctx_in[0:TPH].rearrange("b p d -> p b d")).then_inc(d_ctx, 16)
            sp.dma_start(wq_n[:], Wq.rearrange("(o p) d -> p o d", p=P)).then_inc(d_wq, 16)

            def copy_keys(h):
                sp.wait_ge(job_hi, hn["kv", h] + 1)
                sp.dma_start(k4[QR:2 * QR, :, half(h)].bitcast(F32), k4[0:QR, :, half(h)].bitcast(F32)).then_inc(d_k4[h], 16)

            def copy_queries(h):
                for r in range(R):
                    sp.wait_ge(job_hi, hn["q", h, r // 2] + 2 * (r % 2 + 1))
                    sp.dma_start(q4[2 * QR:3 * QR, :, r, half(h)].bitcast(F32),
                                 q4[0:QR, :, r, half(h)].bitcast(F32)).then_inc(d_q4[h][r], 16)

            sp.wait_ge(d_x, 16)
            sp.dma_start(x_sb[:, TPH:NB, :], x[TPH:NB].rearrange("b p d -> p b d")).then_inc(d_x, 16)
            sp.wait_ge(d_ctx, 16)
            sp.dma_start(c_sb[:, TPH:NB, :], ctx_in[TPH:NB].rearrange("b p d -> p b d")).then_inc(d_ctx, 16)
            sp.dma_start(wo_n[:], Wo.rearrange("(o p) d -> p o d", p=P)).then_inc(d_wo, 16)
            sp.dma_start(rw_n[:], Rw.rearrange("(c p) e -> p c e", p=P)).then_inc(d_rw, 16)
            sp.dma_start(pick_n[:], pick).then_inc(d_pick, 16)
            copy_keys(0)
            copy_queries(0)
            sp.wait_ge(job_done, jn["c", 1, 1] + 1)
            for t in range(FT):
                if t >= WR:
                    sp.wait_ge(w_ok, t - WR + 1)
                s = t % WR
                for m, W in enumerate((Gw, Uw)):
                    for e, f0, f1, at in pieces(t):
                        sp.dma_start(raw_gu[:, s, m, :, at:at + f1 - f0],
                                     W[e, :, f0:f1].rearrange("(c p) f -> p c f", p=P)).then_inc(d_raw[s], 16)
                sp.dma_start(raw_d[:, s], Dw.rearrange("e f d -> (e f) d")[t * P:(t + 1) * P]).then_inc(d_raw[s], 16)
                if t == WR - 1:
                    copy_keys(1)
                    copy_queries(1)
            for y in range(NB // 2):
                sp.wait_ge(fin_ok, y + 1)
                sp.dma_start(out[2 * y:2 * y + 2].rearrange("b p d -> p b d"), x_sb[:, 2 * y:2 * y + 2]).then_inc(d_out, 16)
            sp.wait_ge(d_out, 16 * (NB // 2))

        raw_count = []
        for t in range(FT):
            raw_count.append(16 * (2 * len(pieces(t)) + 1) + (raw_count[t - WR] if t >= WR else 0))

        @block.gpsimd
        def _(pool):
            n_own = [0]

            def step(ins):
                n_own[0] += 1
                ins.then_inc(pool_step, 1)
                pool.wait_ge(pool_step, n_own[0])

            def inverse_deviation(k, t0, n):
                pool.wait_ge(var_ok, k + 1)
                step(pool.tensor_tensor(vare[:, t0:t0 + n], mv[:, t0:t0 + n, 1], cst[:, C_EPS:C_EPS + n], ALU.add))
                pool.tensor_tensor(rstd[:, t0:t0 + n], vare[:, t0:t0 + n], cst[:, C_MH:C_MH + n],
                                   ALU.pow).then_inc(rstd_ok, 1)

            pool.memset(k4[:].bitcast(F32), 1.0)
            pool.memset(zero[:], 0.0).then_inc(pool_init, 1)
            pool.memset(vz[:], 0.0).then_inc(pool_init, 1)
            pool.wait_ge(d_cst, 16)
            inverse_deviation(0, 0, TPH)
            pool.wait_ge(pool_init, 2)
            pool.memset(vz[:, :, :, HD:HD + 1], 1.0)
            pool.memset(mt[:].bitcast(F32), 0.0)
            pool.tensor_copy(ident_b[:], ident).then_inc(pool_init, 1)

            def separate_keys(b):
                if b >= KZ:
                    pool.wait_ge(st_done, G * (b - KZ + 1))
                s = b % KZ
                for hf in range(2):
                    g = slice(GH * hf, GH * (hf + 1))
                    ins = pool.tensor_tensor(
                        kz[0:KR, s, g],
                        k4[0:KR, hf, toks(b)].bitcast(F32).unsqueeze(1).to_broadcast([KR, GH, L]),
                        cst[0:KR, C_G + GH * hf:C_G + GH * (hf + 1)].unsqueeze(2).to_broadcast([KR, GH, L]), ALU.mult)
                    ins.then_inc(kz_ok, 1)

            pool.wait_ge(masks_f, 2)
            pool.tensor_tensor(cmask[:], padf[:].rearrange("p (b k) -> p b k", b=NB),
                               mqk[:].unsqueeze(1).to_broadcast([P, NB, L]), ALU.add).then_inc(mask_ok, 1)
            pool.wait_ge(*emptied(("kv", 0)))
            pool.wait_ge(d_k4[0], 16)
            separate_keys(0)
            inverse_deviation(1, TPH, TPH)
            separate_keys(1)
            separate_keys(2)
            pool.wait_ge(tg_ok, 1)
            pool.wait_ge(d_bo, 16)
            step(pool.tensor_tensor(bo_b[:], bo_b[:], tg[:, 0:1].to_broadcast([P, D]), ALU.mult))
            pool.wait_ge(d_x, 32)
            pool.tensor_tensor(xb_sb[:], x_sb[:], bo_b[:].unsqueeze(1).to_broadcast([P, NB, D]), ALU.add).then_inc(xb_ok, 1)

            def split_weights(t):
                s = t % WR
                pool.wait_ge(d_raw[s], raw_count[t])
                if t == 0:
                    pool.wait_ge(job_done, jn["kv", 1] + 1)
                if t >= WR:
                    pool.wait_ge(y_done, LASTN[t - WR] + 1)
                gu = raw_gu[:, s]
                pool.tensor_tensor(w_gu[0][:, s], gu, zero[:].unsqueeze(2).unsqueeze(3).to_broadcast([P, 2, DC, P]), ALU.add)
                step(pool.tensor_tensor(w_d[0][:, s], raw_d[:, s], zero[:].to_broadcast([P, D]), ALU.add))
                pool.tensor_tensor(w_gu[1][:, s], gu, w_gu[0][:, s].bitcast(F32), ALU.subtract)
                pool.tensor_tensor(w_d[1][:, s], raw_d[:, s], w_d[0][:, s].bitcast(F32), ALU.subtract).then_inc(w_ok, 1)

            for b in range(NB):
                if b + KZ < NB:
                    if b + KZ == TPH:
                        pool.wait_ge(*emptied(("kv", 1)))
                        pool.wait_ge(d_k4[1], 16)
                    separate_keys(b + KZ)
                if b == 1:
                    pool.memset(rw[0][:].bitcast(F32), 0.0)
                    pool.memset(rw[1][:].bitcast(F32), 0.0).then_inc(pool_init, 1)
                    pool.wait_ge(job_done, jn["q", 1, 1] + 1)
                    step(pool.memset(w_t[:, 0:FT * P + NT].bitcast(F32), 0.0))
                    pool.wait_ge(d_pick, 16)
                    pool.tensor_copy(pick_r[0:2 * E], pick_n[:]).then_inc(pick_ok, 1)
                if b in (3, 4):
                    split_weights(b - 3)
                inverse_deviation(NQ + b, b, 1)
            for t in range(WR, FT):
                split_weights(t)

        @block.scalar
        def _(sc):
            sc.dma_start(cst[:], consts).then_inc(d_cst, 16)
            sc.dma_start(wkv_n[0:64, :], Wk).then_inc(d_wkv, 16)
            sc.dma_start(wkv_n[64:128, :], Wv).then_inc(d_wkv, 16)
            for hf in range(2):
                sc.dma_start(bperm[hf * R:(hf + 1) * R, 0:QR].rearrange("r (g d) -> r g d", g=GH),
                             bq.rearrange("(h g r d) -> h r g d", h=2, g=GH, r=R)[hf]).then_inc(d_b, 16)
            sc.dma_start(bperm[2 * R:2 * R + 2, 0:QR], bk.rearrange("(h n) -> h n", h=2)).then_inc(d_b, 16)
            sc.dma_start(bperm[NBC - 1:NBC, :].rearrange("a (u n) -> a u n", u=2),
                         bv.rearrange("(a n) -> a n", a=1).unsqueeze(1).to_broadcast([1, 2, 64])).then_inc(d_b, 16)
            sc.dma_start(gate[:, 0:1], g_x.rearrange("(a n) -> a n", a=1).to_broadcast([P, 1])).then_inc(d_gate, 16)
            sc.dma_start(gate[:, 1:2], g_f.rearrange("(a n) -> a n", a=1).to_broadcast([P, 1])).then_inc(d_gate, 16)
            sc.dma_start(bo_b[:], bo.rearrange("(a n) -> a n", a=1).to_broadcast([P, D])).then_inc(d_bo, 16)
            sc.dma_start(pad_u[:], m_pad.rearrange("(a b) k -> a (b k)", a=1).to_broadcast([P, NB * L])).then_inc(d_mask, 16)
            sc.dma_start(mqk_u[:], m_qk).then_inc(d_mask, 16)

            def high(j, parts=ALL):
                sc.wait_ge(job_done, jn[j] + 1)
                ps, k = jbank(j), j[0]
                if k == "wkv":
                    ins = nc.scalar.copy(wkv[0], ps[:, 0:NKW].rearrange("p (c n) -> p c n", c=DC))
                elif k == "wq":
                    for c in range(DC):
                        ins = nc.scalar.copy(wq[0][:, c].rearrange("p (r g d) -> p r g d", r=R, g=G),
                                             ps[:, c * D:(c + 1) * D].rearrange("p (g r d) -> p r g d", g=G, r=R))
                elif k == "wo":
                    ins = nc.scalar.copy(wo[0][:], ps[:].rearrange("p (c n) -> p c n", c=DC))
                elif k in ("c", "x"):
                    ins = nc.scalar.copy((cT if k == "c" else xT)[0][:, j[2], half(j[1])], ps[:])
                elif k == "kv":
                    if j[1] == 0:
                        sc.wait_ge(pool_init, 1)
                    for hf in range(2):
                        ins = nc.scalar.activation(k4[0:QR, hf, half(j[1])], ps[QR * hf:QR * (hf + 1), :],
                                                   ACT.Identity, bias=bias[QR * hf:QR * (hf + 1), 2 * R + hf:2 * R + hf + 1])
                elif k == "q":
                    for i in parts:
                        hf, r, src = i % 2, 2 * j[2] + i // 2, QR * i
                        ins = nc.scalar.activation(q4[0:QR, hf, r, half(j[1])], ps[src:src + QR, :], ACT.Identity,
                                                   bias=bias[src:src + QR, hf * R + r:hf * R + r + 1])
                        if i != parts[-1]:
                            ins.then_inc(job_hi, 1)
                elif k == "MT":
                    rows = slice(3 * QR, KR)
                    src = ps[rows, :].rearrange("p (r q) -> p r q", r=R)
                    nc.scalar.copy(q4[rows, 0, :, toks(j[1])], src)
                    nc.scalar.copy(q4[rows, 1, :, toks(j[1])], src).then_inc(mt_ok, 1)
                    return
                elif k == "AT":
                    if j[1]:
                        sc.wait_ge(job_done, jn["WO", j[1] - 1] + 1)
                    ins = nc.scalar.copy(aT[0][:], ps[:, 0:D].rearrange("p (c q) -> p c q", c=DC))
                elif k == "YT":
                    ins = nc.scalar.copy(xT[0][:, :, toks(j[1])], ps[:, 0:D].rearrange("p (c q) -> p c q", c=DC))
                ins.then_inc(job_hi, 1)

            for j in PHASE_A:
                if j == ("kv", 0):
                    sc.wait_ge(d_gate, 32)
                    nc.scalar.activation(tg[:], gate[:], ACT.Tanh).then_inc(tg_ok, 1)
                    sc.wait_ge(*emptied(("bias",)))
                if j in hn:
                    high(j)

            high(("MT", 0))

            def copy_o(b, hf):
                sc.wait_ge(pv_done, 2 * b + hf + 1)
                if b:
                    sc.wait_ge(job_done, jn["TO", b - 1, hf] + 1)
                nc.scalar.copy(o_sb[:, hf], bank[4 + hf][:]).then_inc(o_ok, 1)

            def silu(n):
                sc.wait_ge(g_done, n + 1)
                if n >= 2:
                    sc.wait_ge(u_free, n - 1)
                nc.scalar.activation(act_g[:, n % 2], bank[0][:], ACT.Silu).then_inc(a_ok, 1)

            for s in range(SLOTS):
                if s < CH:
                    b, i = s // G, s % G
                    sc.wait_ge(st_done, s + 1)
                    if b and i % 4 == 0:
                        sc.wait_ge(pv_done, 2 * (b - 1) + i // 4 + 1)
                    nc.scalar.activation(pT[:, i // 4, i % 4, :], bank[2 + s % 2][:], ACT.Exp,
                                         scale=SCALE).then_inc(p_done, 1)
                for j, parts in takes_at(s):
                    if j in hn or j[0] == "MT":
                        high(j, parts)
                if s % G == 6 and s < CH:
                    copy_o(s // G, 0)
                if s % G == 1 and G < s < CH + G:
                    copy_o(s // G - 1, 1)
                for h, at in ROUTE.items():
                    if s == at + 4:
                        sc.wait_ge(dif_ok, h + 1)
                        t = slice(h * TPH, (h + 1) * TPH)
                        nc.scalar.activation(e2[:, t], dif[:, t], ACT.Exp).then_inc(e2_ok, 1)
                for n, at in UP_SLOT.items():
                    if s == at + 1:
                        silu(n)
            for n in range(len(UP_SLOT), len(ORDER)):
                silu(n)

        @block.vector
        def _(ve):
            n_own = [0]

            def own(ins):
                n_own[0] += 1
                return ins.then_inc(vec, 1)

            def settle():
                ve.wait_ge(vec, n_own[0])

            def statistics(t0, n):
                for t in range(t0, t0 + n):
                    own(nc.vector.bn_stats(stats[:, t], x_sb[:, t]))
                settle()
                for t in range(t0, t0 + n):
                    ins = nc.vector.bn_aggr(mv[:, t], stats[:, t])
                ins.then_inc(var_ok, 1)

            def normalise(k, t0, n):
                ve.wait_ge(rstd_ok, k + 1)
                for t in range(t0, t0 + n):
                    ins = nc.vector.tensor_scalar(xn[:, t], x_sb[:, t], mv[:, t, 0:1], rstd[:, t:t + 1],
                                                  ALU.subtract, ALU.mult)
                ins.then_inc(xn_ok, 1)

            def minus(dst, ps, hi):
                return nc.vector.tensor_tensor(dst, ps, hi.bitcast(F32), ALU.subtract)

            def minus_biased(dst, ps, col, hi):
                return nc.vector.scalar_tensor_tensor(dst, ps, col, hi.bitcast(F32), ALU.add, ALU.subtract)

            def take(j, parts=ALL):
                ps, k = jbank(j), j[0]
                ve.wait_ge(job_done, jn[j] + 1)
                if j in hn and k != "q":
                    ve.wait_ge(job_hi, hn[j] + 1)
                if k == "bias":
                    ins = nc.vector.tensor_copy(bias[:, 0:NBC], ps[:, 0:NBC])
                elif k == "wkv":
                    ins = minus(wkv[1], ps[:, 0:NKW].rearrange("p (c n) -> p c n", c=DC), wkv[0])
                elif k == "wq":
                    for c in range(DC):
                        ins = minus(wq[1][:, c].rearrange("p (r g d) -> p r g d", r=R, g=G),
                                    ps[:, c * D:(c + 1) * D].rearrange("p (g r d) -> p r g d", g=G, r=R),
                                    wq[0][:, c].rearrange("p (r g d) -> p r g d", r=R, g=G))
                elif k == "wo":
                    ins = minus(wo[1][:], ps[:].rearrange("p (c n) -> p c n", c=DC), wo[0][:])
                elif k in ("c", "x"):
                    t = cT if k == "c" else xT
                    ins = minus(t[1][:, j[2], half(j[1])], ps[:], t[0][:, j[2], half(j[1])])
                elif k == "kv":
                    s = half(j[1])
                    for hf in range(2):
                        minus_biased(k4[2 * QR:3 * QR, hf, s], ps[QR * hf:QR * (hf + 1), :],
                                     bias[0:QR, 2 * R + hf:2 * R + hf + 1], k4[0:QR, hf, s])
                    ins = nc.vector.tensor_scalar(vT[64:128, s], ps[64:128, :], bias[64:128, NBC - 1:NBC], None, ALU.add)
                elif k == "vn":
                    ve.wait_ge(pool_init, 3)
                    ins = nc.vector.tensor_copy(vz[:, j[1] * TPH:(j[1] + 1) * TPH, :, 0:HD],
                                                ps[:, 0:TPH * 64].rearrange("p (b g d) -> p b g d", b=TPH, g=G))
                elif k == "q":
                    for i in parts:
                        ve.wait_ge(job_hi, hn[j] + i + 1)
                        hf, r, src = i % 2, 2 * j[2] + i // 2, QR * i
                        ins = minus_biased(q4[QR:2 * QR, hf, r, half(j[1])], ps[src:src + QR, :],
                                           bias[0:QR, hf * R + r:hf * R + r + 1], q4[0:QR, hf, r, half(j[1])])
                    if parts[-1] != ALL[-1]:
                        return
                elif k == "TO":
                    _, b, hf = j
                    v = ps[:].rearrange("p (r j c) -> p r j c", r=R, c=VW)
                    if b:
                        ve.wait_ge(*emptied(("TO", b - 1, hf)))
                        ve.wait_ge(job_done, jn["AT", b - 1] + 1)
                    own(nc.vector.reciprocal(rden[:, hf], v[:, :, :, HD]))
                    settle()
                    a = an[:, 4 * hf:4 * hf + 4].rearrange("p j r d -> p r j d")
                    ins = nc.vector.tensor_tensor(a, v[:, :, :, 0:HD], rden[:, hf].unsqueeze(3).to_broadcast([P, R, 4, HD]),
                                                  ALU.mult)
                elif k == "AT":
                    ins = minus(aT[1][:], ps[:, 0:D].rearrange("p (c q) -> p c q", c=DC), aT[0][:])
                elif k == "WO":
                    b = j[1]
                    if b == 0:
                        ve.wait_ge(xb_ok, 1)
                    ins = nc.vector.scalar_tensor_tensor(x_sb[:, b], ps[:, 0:D], tg[:, 0:1], xb_sb[:, b], ALU.mult, ALU.add)
                elif k == "YT":
                    s = toks(j[1])
                    ins = minus(xT[1][:, :, s], ps[:, 0:D].rearrange("p (c q) -> p c q", c=DC), xT[0][:, :, s])
                elif k == "SC":
                    ins = nc.vector.tensor_copy(s16[0:E, half(j[1])], ps[0:E, :])
                elif k == "SN":
                    t = slice(j[1] * TPH, (j[1] + 1) * TPH)
                    ins = nc.vector.tensor_copy(sn[:, t], ps[:, 0:TPH * E].rearrange("p (b e) -> p b e", b=TPH))
                elif k == "CT":
                    ins = nc.vector.tensor_copy(cwT[0:2 * E, half(j[1])], ps[0:2 * E, :])
                ins.then_inc(job_lo, 1)
                if k == "WO":
                    ve.wait_ge(*emptied(j))
                    statistics(j[1], 1)

            ve.wait_ge(d_x, 16)
            for t in range(TPH):
                own(nc.vector.bn_stats(stats[:, t], x_sb[:, t]))
            settle()
            for t in range(TPH):
                ins = nc.vector.bn_aggr(mv[:, t], stats[:, t])
            ins.then_inc(var_ok, 1)
            take(("wkv",))
            normalise(0, 0, TPH)
            take(("c", 0, 0))
            take(("c", 0, 1))
            take(("wq",))
            ve.wait_ge(d_b, 64)
            nc.vector.tensor_copy(bperm[0:2 * R + 2, QR:P].rearrange("p (u n) -> p u n", n=QR),
                                  bperm[0:2 * R + 2, 0:QR].unsqueeze(1).to_broadcast([2 * R + 2, P // QR - 1, QR])).then_inc(brow_ok, 1)
            take(("x", 0, 0))
            take(("x", 0, 1))
            take(("bias",))
            ve.wait_ge(d_mask, 32)
            nc.vector.tensor_scalar(mqk[:], mqk_u[:], -BIG, None, ALU.mult).then_inc(masks_f, 1)
            nc.vector.tensor_scalar(padf[:], pad_u[:], -BIG, None, ALU.mult).then_inc(masks_f, 1)
            for j in PHASE_A[7:NA - 1]:
                take(j)
            ve.wait_ge(d_x, 32)
            statistics(TPH, TPH)

            def row_max(n):
                r, hf = n % G // 2, n % 2
                ve.wait_ge(s_done, n + 1)
                if n >= G:
                    ve.wait_ge(m_parts, n // G)
                nc.vector.tensor_reduce(mneg[:, r, 4 * hf:4 * hf + 4], bank[n % 2][:].rearrange("p (g k) -> p g k", g=4),
                                        X, ALU.max, negate=True).then_inc(max_ok, 1)

            def max_parts(b):
                ve.wait_ge(max_ok, G * (b + 1))
                if b:
                    ve.wait_ge(job_done, jn["MT", b - 1] + 1)
                else:
                    ve.wait_ge(pool_init, 3)
                own(nc.vector.tensor_copy(mt[:, :, 3 * QR:3 * QR + G], mneg[:]))
                settle()
                nc.vector.tensor_tensor(mt[:, :, 3 * QR + G:KR], mneg[:], mt[:, :, 3 * QR:3 * QR + G].bitcast(F32), ALU.subtract).then_inc(m_parts, 1)

            def best_two(h):
                ve.wait_ge(*emptied(("SN", h)))
                tiles = range(h * TPH, (h + 1) * TPH)
                t4 = slice(h * TPH, (h + 1) * TPH)
                for t in tiles:
                    own(nc.vector.max(top[:, t], sn[:, t]))
                settle()
                nc.vector.tensor_tensor(dif[:, t4], top[:, t4, 1], top[:, t4, 0], ALU.subtract).then_inc(dif_ok, 1)
                for t in tiles:
                    own(nc.vector.max_index(topi[:, t], top[:, t], sn[:, t]))
                settle()
                own(nc.vector.tensor_copy(topf[:, t4, 0:2], topi[:, t4, 0:2]))

            def two_weights(h):
                t4 = slice(h * TPH, (h + 1) * TPH)
                ve.wait_ge(e2_ok, h + 1)
                own(nc.vector.tensor_scalar(den2[:, t4], e2[:, t4], 1.0, None, ALU.add))
                settle()
                own(nc.vector.reciprocal(w1[:, t4], den2[:, t4]))
                settle()
                own(nc.vector.tensor_scalar(w1[:, t4], w1[:, t4], tg[:, 1:2], None, ALU.mult))
                settle()
                own(nc.vector.tensor_tensor(w2[:, t4], w1[:, t4], e2[:, t4], ALU.mult))
                settle()

            def expert_weights(h):
                t4 = slice(h * TPH, (h + 1) * TPH)
                iota = cst[:, C_IOTA:C_IOTA + E]
                for t in range(h * TPH, (h + 1) * TPH):
                    own(nc.vector.tensor_scalar(cb1[:, t], iota, topf[:, t, 0:1], w1[:, t:t + 1], ALU.is_equal, ALU.mult))
                    own(nc.vector.tensor_scalar(cb2[:, t], iota, topf[:, t, 1:2], w2[:, t:t + 1], ALU.is_equal, ALU.mult))
                settle()
                own(nc.vector.tensor_tensor(comb[:, t4], cb1[:, t4], cb2[:, t4], ALU.add))
                settle()
                own(nc.vector.tensor_copy(c2[:, t4, 0], comb[:, t4]))
                settle()
                nc.vector.tensor_tensor(c2[:, t4, 1], comb[:, t4], c2[:, t4, 0].bitcast(F32), ALU.subtract).then_inc(c2_ok, 1)

            def hidden(n):
                ve.wait_ge(a_ok, n + 1)
                ve.wait_ge(u_done, n + 1)
                if n == 0:
                    ve.wait_ge(pv_done, 2 * NB)
                nc.vector.tensor_tensor(h_su, act_g[:, n % 2], bank[1][:], ALU.mult).then_inc(u_free, 1)
                j = ("CB", n)
                ve.wait_ge(u_free, n + 1)
                ve.wait_ge(job_done, jn[j] + 1)
                if n:
                    ve.wait_ge(h_ok, n)
                nc.vector.tensor_tensor(h_all, h_su, jbank(j)[:], ALU.mult).then_inc(job_lo, 1)
                ve.wait_ge(*emptied(j))
                if n >= 2:
                    ve.wait_ge(y_done, n - 1)
                own(nc.vector.tensor_copy(hh[:, n % 2], h_all))
                settle()
                nc.vector.tensor_tensor(hl[:, n % 2], h_all, hh[:, n % 2].bitcast(F32), ALU.subtract).then_inc(h_ok, 1)

            for n in range(G):
                row_max(n)
            max_parts(0)
            for n in range(G, LEAD):
                row_max(n)
            normalise(1, TPH, TPH)
            for s in range(SLOTS):
                if s + LEAD < CH:
                    row_max(s + LEAD)
                    if (s + LEAD) % G == G - 1:
                        max_parts((s + LEAD) // G)
                if s == 20:
                    ve.wait_ge(pool_init, 4)
                    ve.wait_ge(d_rw, 16)
                    own(nc.vector.tensor_copy(rw[0][:, :, 0:E], rw_n[:]))
                    settle()
                    nc.vector.tensor_tensor(rw[1][:, :, 0:E], rw_n[:], rw[0][:, :, 0:E].bitcast(F32), ALU.subtract).then_inc(rw_ok, 1)
                for j, parts in takes_at(s):
                    if j[0] == "CB":
                        hidden(j[1])
                    elif j[0] != "MT":
                        take(j, parts)
                if s % G == 2 and 2 * G <= s < 2 * G + CH:
                    b = s // G - 2
                    normalise(NQ + b, b, 1)
                for h, at in ROUTE.items():
                    if s == at + 3:
                        best_two(h)
                    if s == at + 5:
                        two_weights(h)
                    if s == at + 6:
                        expert_weights(h)
            for n in range(len(CB_SLOT), len(ORDER)):
                hidden(n)
                if n >= len(ORDER) - 1:
                    for y in range(NB // 2):
                        if y % 2 == 0:
                            ve.wait_ge(y_done, len(ORDER) - 1 + y // 2)
                        for t in (2 * y, 2 * y + 1):
                            ins = nc.vector.tensor_tensor(x_sb[:, t], bank[2 + y][:, t % 2 * D:(t % 2 + 1) * D], x_sb[:, t], ALU.add)
                        ins.then_inc(fin_ok, 1)

        @block.tensor
        def _(pe):
            def mm(dst, a, b, start, stop):
                return nc.tensor.matmul(dst, a, b, start=start, stop=stop, skip_group_check=True)

            def three(dst, st, mv_, chunks, first=True):
                terms = [(st[0], mv_[0]), (st[0], mv_[1]), (st[1], mv_[0])]
                last = None
                for c in range(chunks):
                    for k, (a, b) in enumerate(terms):
                        last = mm(dst, a(c), b(c), first and c == 0 and k == 0, c == chunks - 1 and k == 2)
                return last

            def job(j):
                if before(j) is not None:
                    pe.wait_ge(*emptied(before(j)))
                ps, k = jbank(j), j[0]
                if k == "bias":
                    pe.wait_ge(brow_ok, 1)
                    pe.wait_ge(d_cst, 16)
                    ins = nc.tensor.transpose(ps[:, 0:NBC], bperm[:], ident[0:NBC, 0:NBC])
                elif k == "wkv":
                    pe.wait_ge(d_wkv, 32)
                    for c in range(DC):
                        ins = nc.tensor.transpose(ps[:, c * P:(c + 1) * P], wkv_n[:, c * P:(c + 1) * P], ident)
                elif k in ("wq", "wo"):
                    src = wq_n if k == "wq" else wo_n
                    pe.wait_ge(d_wq if k == "wq" else d_wo, 16)
                    for c in range(DC):
                        for o in range(DC):
                            ins = nc.tensor.transpose(ps[:, c * D + o * P:c * D + (o + 1) * P],
                                                      src[:, o, c * P:(c + 1) * P], ident)
                elif k in ("c", "x"):
                    _, h, c = j
                    if k == "c":
                        pe.wait_ge(d_ctx, 16 * (h + 1))
                    else:
                        pe.wait_ge(xn_ok, h + 1)
                    src = c_sb if k == "c" else xn
                    for t in range(TPH):
                        ins = nc.tensor.transpose(ps[:, toks(t)], src[:, h * TPH + t, c * P:(c + 1) * P], ident)
                elif k == "vn":
                    pe.wait_ge(*emptied(("kv", j[1])))
                    for b in range(TPH):
                        ins = nc.tensor.transpose(ps[:, b * 64:(b + 1) * 64], vT[64:128, toks(j[1] * TPH + b)],
                                                  ident[64:128, 64:128])
                elif k == "kv":
                    pe.wait_ge(*emptied(("c", j[1], 1)))
                    ins = three(ps[:], [lambda c, i=i: wkv[i][:, c] for i in range(2)],
                                [lambda c, i=i: cT[i][:, c, half(j[1])] for i in range(2)], DC)
                elif k == "q":
                    pe.wait_ge(*emptied(("x", j[1], 1)))
                    ins = three(ps[:], [lambda c, i=i: wq[i][:, c, j[2] * P:(j[2] + 1) * P] for i in range(2)],
                                [lambda c, i=i: xT[i][:, c, half(j[1])] for i in range(2)], DC)
                elif k == "MT":
                    pe.wait_ge(m_parts, j[1] + 1)
                    for r in range(R):
                        ins = nc.tensor.transpose(ps[0:KR, r * L:(r + 1) * L], mt[:, r].bitcast(F32), ident)
                elif k == "TO":
                    pe.wait_ge(o_ok, 2 * j[1] + j[2] + 1)
                    for r in range(R):
                        ins = nc.tensor.transpose(ps[:, r * P:(r + 1) * P], o_sb[:, j[2], r * L:(r + 1) * L], ident)
                elif k == "AT":
                    pe.wait_ge(*emptied(("TO", j[1], 1)))
                    a = an[:].rearrange("p g r d -> p (g r d)")
                    for c in range(DC):
                        ins = nc.tensor.transpose(ps[:, c * L:(c + 1) * L], a[:, c * P:(c + 1) * P], ident)
                elif k == "WO":
                    pe.wait_ge(*emptied(("AT", j[1])))
                    ins = three(ps[:, 0:D], [lambda c, i=i: aT[i][:, c] for i in range(2)],
                                [lambda c, i=i: wo[i][:, c] for i in range(2)], DC)
                elif k == "YT":
                    pe.wait_ge(xn_ok, NQ + j[1] + 1)
                    for c in range(DC):
                        ins = nc.tensor.transpose(ps[:, c * L:(c + 1) * L], xn[:, j[1], c * P:(c + 1) * P], ident)
                elif k == "SC":
                    pe.wait_ge(*emptied(("YT", (j[1] + 1) * TPH - 1)))
                    pe.wait_ge(rw_ok, 1)
                    ins = three(ps[:], [lambda c, i=i: rw[i][:, c] for i in range(2)],
                                [lambda c, i=i: xT[i][:, c, half(j[1])] for i in range(2)], DC)
                elif k == "SN":
                    pe.wait_ge(*emptied(("SC", j[1])))
                    for t in range(TPH):
                        ins = nc.tensor.transpose(ps[:, t * E:(t + 1) * E], s16[0:E, toks(j[1] * TPH + t)], ident[0:E, 0:E])
                elif k == "CT":
                    pe.wait_ge(c2_ok, j[1] + 1)
                    for t in range(TPH):
                        ins = nc.tensor.transpose(ps[0:2 * E, toks(t)],
                                                  c2[:, j[1] * TPH + t].rearrange("p a e -> p (a e)").bitcast(F32), ident)
                elif k == "CB":
                    t, h = ORDER[j[1]]
                    pe.wait_ge(*emptied(("CT", h)))
                    pe.wait_ge(pick_ok, 1)
                    ins = mm(ps[:], pick_r[:, t * P:(t + 1) * P], cwT[:, half(h)], True, True)
                ins.then_inc(job_done, 1)

            for j in PHASE_A[:NA - 1]:
                job(j)

            def scores_q(n):
                b, r, hf = n // G, n % G // 2, n % 2
                if n >= 2:
                    pe.wait_ge(max_ok, n - 1)
                if n % G == 0:
                    pe.wait_ge(kz_ok, 2 * (b + 1))
                if b % TPH == 0 and hf == 0:
                    pe.wait_ge(*emptied(("q", b // TPH, r // 2)))
                    pe.wait_ge(d_q4[b // TPH][r], 16)
                s, g4, ps = b % KZ, slice(4 * hf, 4 * hf + 4), bank[n % 2]
                mm(ps[:], q4[0:3 * QR, hf, r, toks(b)], kz[0:3 * QR, s, g4].rearrange("p g k -> p (g k)"), True, False)
                mm(ps[:], ident_b[:], cmask[:, b].unsqueeze(1).to_broadcast([P, 4, L]), False, True).then_inc(s_done, 1)

            def scores_k(n):
                b, g = n // G, n % G
                if n >= 2:
                    pe.wait_ge(p_done, n - 1)
                if g == 0:
                    pe.wait_ge(*emptied(("MT", b)))
                s, ps = b % KZ, bank[2 + n % 2][:].rearrange("p (r q) -> p r q", r=R)
                mm(ps, cmask[:, b], ident_b[:].unsqueeze(1).to_broadcast([P, R, L]), True, False)
                mm(ps, kz[0:KR, s, g], q4[0:KR, g // GH, :, toks(b)], False, True).then_inc(st_done, 1)

            def weigh_values(b, hf):
                pe.wait_ge(p_done, G * b + 4 * hf + 4)
                if b:
                    pe.wait_ge(o_ok, 2 * (b - 1) + hf + 1)
                for j in range(4):
                    ins = mm(bank[4 + hf][VW * j:VW * (j + 1), :], vz[:, b, 4 * hf + j], pT[:, hf, j], True, True)
                ins.then_inc(pv_done, 1)

            def up(n):
                t, h = ORDER[n]
                s = t % WR
                pe.wait_ge(w_ok, t + 1)
                pe.wait_ge(*emptied(("YT", (h + 1) * TPH - 1)))
                if n == 0:
                    pe.wait_ge(max_ok, CH)
                for m, done, free in ((0, g_done, a_ok), (1, u_done, u_free)):
                    if n:
                        pe.wait_ge(free, n)
                    three(bank[m][:], [lambda c, i=i: w_gu[i][:, s, m, c] for i in range(2)],
                          [lambda c, i=i: xT[i][:, c, half(h)] for i in range(2)], DC).then_inc(done, 1)

            def down(n):
                t, h = ORDER[n]
                s = t % WR
                pe.wait_ge(h_ok, n + 1)
                if n == 0:
                    pe.wait_ge(p_done, CH)
                    pe.wait_ge(o_ok, 2 * NB)
                for u in range(TPH):
                    ins = three(bank[2 + (h * TPH + u) // 2][:, u % 2 * D:(u % 2 + 1) * D],
                                [lambda c, i=i: (hh, hl)[i][:, n % 2, toks(u)] for i in range(2)],
                                [lambda c, i=i: w_d[i][:, s] for i in range(2)], 1, first=(t == 0 and u % 2 == 0))
                ins.then_inc(y_done, 1)

            pe.wait_ge(mask_ok, 1)
            pe.wait_ge(pool_init, 3)
            for n in range(LEAD):
                scores_q(n)
                if n == G + 1:
                    job(("MT", 0))
            for s in range(SLOTS):
                if s < CH:
                    scores_k(s)
                if s + LEAD < CH:
                    scores_q(s + LEAD)
                if s % G == 5 and s < CH:
                    weigh_values(s // G, 0)
                if s % G == 0 and 0 < s <= CH:
                    weigh_values(s // G - 1, 1)
                for j in jobs_at(s):
                    job(j)
                for n, at in UP_SLOT.items():
                    if s == at:
                        up(n)
                for n, at in DOWN_SLOT.items():
                    if s == at:
                        down(n)
            first = len(DOWN_SLOT)
            for n in range(first, len(ORDER)):
                job(("CB", n))
                if n + 1 < len(ORDER):
                    up(n + 1)
                down(n)


_INS = ['x', 'ctx_2048', 'mask_SxS2_bc0', 'mask_BxS2_bk0', 'g_xattn', 'g_ffn', 'L0_xattn_Wq', 'L0_xattn_bq',
        'L0_xattn_Wk', 'L0_xattn_bk', 'L0_xattn_Wv', 'L0_xattn_bv', 'L0_xattn_Wo', 'L0_xattn_bo',
        'L0_ffn_router_w', 'L0_ffn_gate_w', 'L0_ffn_up_w', 'L0_ffn_down_w']


def kernel(**inputs):
    import concourse.bacc as _bacc
    from concourse.bass_utils import run_bass_kernel_spmd as _run

    nc = _bacc.Bacc("TRN2", target_bir_lowering=False, num_devices=1)
    arrays, args = {}, []
    for name in _INS:
        a = np.ascontiguousarray(inputs[name])
        arrays[f"in_{name}"] = a
        args.append(nc.dram_tensor(f"in_{name}", a.shape, mybir.dt.from_np(a.dtype), kind="ExternalInput").ap())
    c = shape_constants()
    arrays["shape_constants"] = c
    args.append(nc.dram_tensor("shape_constants", c.shape, F32, kind="ExternalInput").ap())
    c = expert_rows()
    arrays["expert_rows"] = c
    args.append(nc.dram_tensor("expert_rows", c.shape, U8, kind="ExternalInput").ap())
    args.append(nc.dram_tensor("out_0", (NB, L, D), F32, kind="ExternalOutput").ap())
    build(nc, *args)
    r = _run(nc, [arrays], core_ids=[0])
    return r.results[0]["out_0"]
```

```python
import numpy as np
from contextlib import ExitStack

import concourse.bass as bass
from concourse import mybir

P = 128
NB = 8
L = 128
NT = NB * L
D = 256
DC = D // P
HD = 8
G = 8
R = 4
GH = G // 2
QR = GH * HD
NQ = 2
TH = NT // NQ
TPH = NB // NQ
E = 16
F = 96
EPS = 1e-5
BIG = float(2 ** 100)
SCALE = 1.0 / float(np.sqrt(np.float32(HD)))
VW = 32
KR = 3 * QR + 2 * G
KZ = 3
LEAD = 12
CH = NB * G
FT = E * F // P
UL = 3
WR = 3
GUC = 2 * DC * P

C_ID, C_G, C_IOTA, C_EPS, C_MH, C_E, C_N = 0, 128, 144, 160, 168, 176, 180

F32 = mybir.dt.float32
F32R = mybir.dt.float32r
BF16 = mybir.dt.bfloat16
U8 = mybir.dt.uint8
U32 = mybir.dt.uint32
ALU = mybir.AluOpType
ACT = mybir.ActivationFunctionType
X = mybir.AxisListType.X


def shape_constants():
    c = np.zeros((P, C_N), np.float32)
    p = np.arange(P)[:, None]
    g = np.arange(G)[None, :]
    c[:, C_ID:C_ID + P] = np.eye(P)
    score = (p % QR // HD == g % GH) & (p < 3 * QR)
    maxima = ((p - 3 * QR) % G == g) & (p >= 3 * QR) & (p < KR)
    c[:, C_G:C_G + G] = score | maxima
    c[:, C_IOTA:C_IOTA + E] = np.arange(E)
    c[:, C_EPS:C_EPS + NB] = EPS
    c[:, C_MH:C_MH + NB] = -0.5
    c[:, C_E:C_E + TPH] = np.e
    return c


def expert_rows():
    e = np.arange(2 * E)[:, None] % E
    return (np.arange(FT * P)[None, :] // F == e).astype(np.bool_)


def build(nc, x, ctx_in, m_qk, m_pad, g_x, g_f, Wq, bq, Wk, bk, Wv, bv, Wo, bo, Rw, Gw, Uw, Dw, consts, pick, out):
    es = ExitStack()
    with es:
        def sb(name, shape, dt=F32):
            return es.enter_context(nc.sbuf_tensor(name, shape, dt))

        def sem(name):
            return es.enter_context(nc.semaphore(name))

        cst = sb("cst", [P, C_N])
        ident = cst[:, C_ID:C_ID + P]
        ident_b = sb("ident_b", [P, P], BF16)
        x_sb = sb("x_sb", [P, NB, D])
        xb_sb = sb("xb_sb", [P, NB, D])
        c_sb = sb("c_sb", [P, NB, D])
        xn = sb("xn", [P, NB, D])
        wq_n = sb("wq_n", [P, DC, D])
        wkv_n = sb("wkv_n", [P, D])
        wo_n = sb("wo_n", [P, DC, D])
        NQW, NKW = DC * D, DC * P
        w_t = sb("w_t", [P, FT * P + NT], F32R)
        wq = [w_t[:, i * NQW:(i + 1) * NQW].rearrange("p (c n) -> p c n", c=DC) for i in range(2)]
        wkv = [w_t[:, 2 * NQW + i * NKW:2 * NQW + (i + 1) * NKW].rearrange("p (c n) -> p c n", c=DC) for i in range(2)]
        wo = [sb(f"wo{i}", [P, DC, D], F32R) for i in range(2)]
        rw_n = sb("rw_n", [P, DC, E])
        rw = [sb(f"rw{i}", [P, DC, P], F32R) for i in range(2)]
        xT = [sb(f"xT{i}", [P, DC, NT], F32R) for i in range(2)]
        cT = [sb(f"cT{i}", [P, DC, NT], F32R) for i in range(2)]
        NBC = 2 * R + 3
        bperm = sb("bperm", [NBC, P])
        bias = sb("bias", [P, 16])
        q4 = sb("q4", [P, 2, R, NT], F32R)
        k4 = sb("k4", [P, 2, NT], F32R)
        kz = sb("kz", [P, KZ, G, L], F32R)
        vT = sb("vT", [P, NT])
        vz = sb("vz", [P, NB, G, VW])
        mqk_u = sb("mqk_u", [P, L], U8)
        pad_u = sb("pad_u", [P, NB * L], U8)
        mqk = sb("mqk", [P, L])
        padf = sb("padf", [P, NB * L])
        cmask = sb("cmask", [P, NB, L], BF16)
        bo_b = sb("bo_b", [P, D])
        gate = sb("gate", [P, 2])
        tg = sb("tg", [P, 2])
        stats = sb("stats", [P, NB, 6])
        mv = sb("mv", [P, NB, 2])
        vare = sb("vare", [P, NB])
        rstd = sb("rstd", [P, NB])
        mneg = sb("mneg", [P, R, G])
        mt = sb("mt", [P, R, KR], F32R)
        pT = sb("pT", [P, 2, G // 2, R * L])
        o_sb = sb("o_sb", [P, 2, R * L])
        rden = sb("rden", [P, 2, R, G // 2])
        an = sb("an", [P, G, R, HD])
        aT = [sb(f"aT{i}", [P, DC, L], F32R) for i in range(2)]
        s16 = vT
        sn = sb("sn", [P, NB, E])
        top = sb("top", [P, NB, 8])
        topi = sb("topi", [P, NB, 8], U32)
        topf = sb("topf", [P, NB, 8])
        dif = sb("dif", [P, NB])
        e2 = sb("e2", [P, NB])
        den2 = sb("den2", [P, NB])
        inv2 = sb("inv2", [P, NB])
        w1 = sb("w1", [P, NB])
        w2 = sb("w2", [P, NB])
        cb1 = sb("cb1", [P, NB, E])
        cb2 = sb("cb2", [P, NB, E])
        comb = sb("comb", [P, NB, E])
        p_flat = pT[:].rearrange("p h j n -> p (h j n)")
        q_flat = q4[:].rearrange("p h r n -> p (h r n)")
        act_g = p_flat[:, 0:2 * TH].rearrange("p (s n) -> p s n", s=2)
        h_su = p_flat[:, 2 * TH:(2 + UL) * TH].rearrange("p (s n) -> p s n", s=UL)
        h_all = p_flat[:, (2 + UL) * TH:(3 + UL) * TH]
        hh = q_flat[:, 0:2 * TH].rearrange("p (s n) -> p s n", s=2)
        hl = q_flat[:, 2 * TH:4 * TH].rearrange("p (s n) -> p s n", s=2)
        c2 = sb("c2", [P, NB, 2, E], F32R)
        pick_n = sb("pick_n", [2 * E, FT * P], U8)
        pick_r = w_t[:, 0:FT * P]
        cwT = w_t[:, FT * P:FT * P + NT]
        zero = sb("zero", [P, 1])
        def gu_view(t, flat):
            return t[:].rearrange(flat)[:, 0:WR * GUC].rearrange("p (s m c f) -> p s m c f", s=WR, m=2, c=DC)

        raw_gu = gu_view(c_sb, "p b d -> p (b d)")
        w_gu = [gu_view(t, "p c n -> p (c n)") for t in cT]
        raw_d = padf[:, 0:WR * D].rearrange("p (s n) -> p s n", s=WR)
        w_d = [sb(f"w_d{i}", [P, WR, D], F32R) for i in range(2)]

        bank = [es.enter_context(nc.psum_tensor(f"bank{i}", [P, 512], F32)) for i in range(8)]

        d_cst, d_wkv, d_wq, d_wo, d_ctx, d_x, d_b, d_bo, d_mask, d_gate, d_rw, d_pick = (
            sem(n) for n in ("d_cst", "d_wkv", "d_wq", "d_wo", "d_ctx", "d_x", "d_b", "d_bo", "d_mask", "d_gate",
                             "d_rw", "d_pick"))
        d_x0 = sem("d_x0")
        d_raw = [sem(f"d_raw{i}") for i in range(WR)]
        d_out = sem("d_out")
        pool_init = sem("pool_init")
        pool_step = sem("pool_step")
        mask_ok = sem("mask_ok")
        xb_ok = sem("xb_ok")
        kz_ok = sem("kz_ok")
        pick_ok = sem("pick_ok")
        var_ok = sem("var_ok")
        rstd_ok = sem("rstd_ok")
        xn_ok = sem("xn_ok")
        brow_ok = sem("brow_ok")
        d_q4 = [[sem(f"d_q4_{h}_{r}") for r in range(R)] for h in range(NQ)]
        job_done = sem("job_done")
        job_hi = sem("job_hi")
        job_lo = sem("job_lo")
        q_lo = sem("q_lo")
        k_ok = sem("k_ok")
        v_ok = sem("v_ok")
        mt_ok = sem("mt_ok")
        s_done = sem("s_done")
        max_ok = sem("max_ok")
        m_parts = sem("m_parts")
        st_done = sem("st_done")
        p_done = sem("p_done")
        pv_done = sem("pv_done")
        o_ok = sem("o_ok")
        masks_f = sem("masks_f")
        rw_ok = sem("rw_ok")
        vec = sem("vec")
        tg_ok = sem("tg_ok")
        dif_ok, e2_ok, c2_ok = sem("dif_ok"), sem("e2_ok"), sem("c2_ok")
        w_ok = sem("w_ok")
        wd_ok = sem("wd_ok")
        g_done = sem("g_done")
        u_done = sem("u_done")
        u_free = sem("u_free")
        a_ok = sem("a_ok")
        h_ok = sem("h_ok")
        y_done = sem("y_done")
        fin_ok = sem("fin_ok")

        PHASE_A = [("wkv",), ("c", 0, 0), ("c", 0, 1), ("wq",), ("x", 0, 0), ("x", 0, 1), ("bias",), ("kv", 0),
                   ("q", 0, 0), ("q", 0, 1), ("c", 1, 0), ("c", 1, 1), ("MT", 0)]
        AT_SLOT = {("vn", 0): 0, ("wo",): 8, ("x", 1, 0): 5, ("x", 1, 1): 6,
                   ("kv", 1): 3, ("q", 1, 0): 8, ("q", 1, 1): 11, ("vn", 1): 16}
        NORM_SLOT = {}
        for b in range(NB):
            if b:
                AT_SLOT["MT", b] = G * b - 3
            at = {0: (7, 10, 13, 15, 18, 19), NB - 1: (7, 9, 10, 12, 14, 15)}.get(b, (7, 10, 12, 14, 18, 19))
            for j, k in zip((("TO", b, 0), ("TO", b, 1), ("AT", b), ("WO", b), None, ("YT", b)), at):
                if j:
                    AT_SLOT[j] = G * b + k
                else:
                    NORM_SLOT[b] = G * b + k
        ROUTE = {"SC": (48, 73), "SN": (49, 75), "best": (51, 76), "weights": (53, 77), "CT": (55, 78)}
        for k in ("SC", "SN", "CT"):
            for h in range(NQ):
                AT_SLOT[k, h] = ROUTE[k][h]
        ORDER = [(t, h) for h in range(NQ) for t in range(WR)] + [(t, h) for t in range(WR, FT) for h in range(NQ)]
        LASTN = {t: max(n for n, (u, _) in enumerate(ORDER) if u == t) for t in range(FT)}
        UP_SLOT = {0: 64, 1: 66, 2: 70, 3: 74, 4: 76, 5: 78}
        CB_SLOT = {0: 65, 1: 69, 2: 71, 3: 79}
        DOWN_SLOT = {0: 68, 1: 71, 2: 76}
        SLOTS = 82
        for n, s in CB_SLOT.items():
            AT_SLOT["CB", n] = s
        LATER = sorted(AT_SLOT, key=lambda j: AT_SLOT[j])
        LATER += [("CB", n) for n in range(len(CB_SLOT), len(ORDER))]
        JOBS = PHASE_A + LATER
        NA = len(PHASE_A)
        jn = {j: n for n, j in enumerate(JOBS)}
        ALL = (0, 1, 2, 3)
        hn, count = {}, 0
        for j in JOBS:
            if j[0] in ("wkv", "wq", "wo", "c", "x", "kv", "q", "AT", "YT"):
                hn[j] = count
                count += {"q": 4, "kv": 2}.get(j[0], 1)
        ln = {j: n for n, j in enumerate(j for j in JOBS if j[0] not in ("MT", "q", "kv"))}

        def emptied(j):
            if j[0] == "MT":
                return mt_ok, j[1] + 1
            if j[0] == "q":
                return q_lo, R * j[1] + 2 * (j[2] + 1)
            if j[0] == "kv":
                return k_ok, 2 * (j[1] + 1)
            return job_lo, ln[j] + 1

        BANK = {j: 2 + n % 6 if n < NA else 6 + n % 2 for n, j in enumerate(JOBS)}

        def jbank(j):
            return bank[BANK[j]]

        def before(j):
            same = [k for k in JOBS[:jn[j]] if BANK[k] == BANK[j]]
            return same[-1] if same else None

        def issued(s):
            return min(CH, LEAD + s + 1)

        def ahead(s):
            return range(issued(s - 1), issued(s))

        def jobs_at(s):
            return [j for j in LATER if AT_SLOT.get(j) == s]

        def takes_at(s):
            return ([(j, (2, 3)) for j in jobs_at(s - 2) if j[0] == "q"] +
                    [(j, (0, 1) if j[0] == "q" else ALL) for j in jobs_at(s - 1)])

        def toks(t):
            return slice(t * L, (t + 1) * L)

        def half(h):
            return slice(h * TH, (h + 1) * TH)

        def pieces(t):
            out_, at = [], P * t
            while at < P * (t + 1):
                e = at // F
                n = min((e + 1) * F, P * (t + 1)) - at
                out_.append((e, at - e * F, at - e * F + n, at - P * t))
                at += n
            return out_

        block = es.enter_context(nc.Block())

        @block.sync
        def _(sp):
            sp.dma_start(x_sb[:, 0:2, :], x[0:2].rearrange("b p d -> p b d")).then_inc(d_x0, 16)
            sp.dma_start(x_sb[:, 2:TPH, :], x[2:TPH].rearrange("b p d -> p b d")).then_inc(d_x, 16)
            sp.dma_start(c_sb[:, 0:TPH, :], ctx_in[0:TPH].rearrange("b p d -> p b d")).then_inc(d_ctx, 16)
            sp.dma_start(wq_n[:], Wq.rearrange("(o p) d -> p o d", p=P)).then_inc(d_wq, 16)
            for hf in range(2):
                sp.dma_start(bperm[hf * R:(hf + 1) * R, 0:QR].rearrange("r (g d) -> r g d", g=GH),
                             bq.rearrange("(h g r d) -> h r g d", h=2, g=GH, r=R)[hf]).then_inc(d_b, 16)
            sp.dma_start(bperm[2 * R:2 * R + 2, 0:QR], bk.rearrange("(h n) -> h n", h=2)).then_inc(d_b, 16)
            sp.dma_start(bperm[NBC - 1:NBC, :].rearrange("a (u n) -> a u n", u=2),
                         bv.rearrange("(a n) -> a n", a=1).unsqueeze(1).to_broadcast([1, 2, 64])).then_inc(d_b, 16)
            sp.dma_start(gate[:, 0:1], g_x.rearrange("(a n) -> a n", a=1).to_broadcast([P, 1])).then_inc(d_gate, 16)
            sp.dma_start(gate[:, 1:2], g_f.rearrange("(a n) -> a n", a=1).to_broadcast([P, 1])).then_inc(d_gate, 16)
            sp.dma_start(bo_b[:], bo.rearrange("(a n) -> a n", a=1).to_broadcast([P, D])).then_inc(d_bo, 16)
            sp.dma_start(pad_u[:], m_pad.rearrange("(a b) k -> a (b k)", a=1).to_broadcast([P, NB * L])).then_inc(d_mask, 16)
            sp.dma_start(mqk_u[:], m_qk).then_inc(d_mask, 16)

            def copy_queries(h):
                for r in range(R):
                    sp.wait_ge(job_hi, hn["q", h, r // 2] + 2 * (r % 2 + 1))
                    sp.dma_start(q4[2 * QR:3 * QR, :, r, half(h)].bitcast(F32),
                                 q4[0:QR, :, r, half(h)].bitcast(F32)).then_inc(d_q4[h][r], 16)

            sp.wait_ge(d_x, 16)
            sp.dma_start(x_sb[:, TPH:NB, :], x[TPH:NB].rearrange("b p d -> p b d")).then_inc(d_x, 16)
            sp.wait_ge(d_ctx, 16)
            sp.dma_start(c_sb[:, TPH:NB, :], ctx_in[TPH:NB].rearrange("b p d -> p b d")).then_inc(d_ctx, 16)
            sp.dma_start(wo_n[:], Wo.rearrange("(o p) d -> p o d", p=P)).then_inc(d_wo, 16)
            sp.dma_start(rw_n[:], Rw.rearrange("(c p) e -> p c e", p=P)).then_inc(d_rw, 16)
            sp.dma_start(pick_n[:], pick).then_inc(d_pick, 16)
            copy_queries(0)
            sp.wait_ge(job_done, jn["c", 1, 1] + 1)
            sp.wait_ge(mask_ok, 1)
            for t in range(FT):
                if t >= WR:
                    sp.wait_ge(wd_ok, t - WR + 1)
                s = t % WR
                for m, W in enumerate((Gw, Uw)):
                    for e, f0, f1, at in pieces(t):
                        sp.dma_start(raw_gu[:, s, m, :, at:at + f1 - f0],
                                     W[e, :, f0:f1].rearrange("(c p) f -> p c f", p=P)).then_inc(d_raw[s], 16)
                sp.dma_start(raw_d[:, s], Dw.rearrange("e f d -> (e f) d")[t * P:(t + 1) * P]).then_inc(d_raw[s], 16)
                if t == WR - 1:
                    copy_queries(1)
            for y in range(NB // 2):
                sp.wait_ge(fin_ok, y + 1)
                sp.dma_start(out[2 * y:2 * y + 2].rearrange("b p d -> p b d"), x_sb[:, 2 * y:2 * y + 2]).then_inc(d_out, 16)
            sp.wait_ge(d_out, 16 * (NB // 2))

        raw_count = []
        for t in range(FT):
            raw_count.append(16 * (2 * len(pieces(t)) + 1) + (raw_count[t - WR] if t >= WR else 0))

        @block.gpsimd
        def _(pool):
            n_own = [0]

            def step(ins):
                n_own[0] += 1
                ins.then_inc(pool_step, 1)
                pool.wait_ge(pool_step, n_own[0])

            def inverse_deviation(k, t0, n):
                pool.wait_ge(var_ok, k + 1)
                step(pool.tensor_tensor(vare[:, t0:t0 + n], mv[:, t0:t0 + n, 1], cst[:, C_EPS:C_EPS + n], ALU.add))
                pool.tensor_tensor(rstd[:, t0:t0 + n], vare[:, t0:t0 + n], cst[:, C_MH:C_MH + n],
                                   ALU.pow).then_inc(rstd_ok, 1)

            pool.memset(k4[:].bitcast(F32), 1.0)
            pool.memset(zero[:], 0.0).then_inc(pool_init, 1)
            pool.memset(vz[:], 0.0).then_inc(pool_init, 1)
            pool.wait_ge(d_cst, 16)
            inverse_deviation(0, 0, TPH)
            pool.wait_ge(pool_init, 2)
            pool.memset(vz[:, :, :, HD:HD + 1], 1.0)
            pool.memset(mt[:].bitcast(F32), 0.0)
            pool.tensor_copy(ident_b[:], ident).then_inc(pool_init, 1)

            def separate_keys(b):
                if b >= KZ:
                    pool.wait_ge(st_done, G * (b - KZ + 1))
                s = b % KZ
                for hf in range(2):
                    if b == 0:
                        pool.wait_ge(k_ok, hf + 1)
                    g = slice(GH * hf, GH * (hf + 1))
                    ins = pool.tensor_tensor(
                        kz[0:KR, s, g],
                        k4[0:KR, hf, toks(b)].bitcast(F32).unsqueeze(1).to_broadcast([KR, GH, L]),
                        cst[0:KR, C_G + GH * hf:C_G + GH * (hf + 1)].unsqueeze(2).to_broadcast([KR, GH, L]), ALU.mult)
                    ins.then_inc(kz_ok, 1)

            pool.wait_ge(masks_f, 2)
            pool.tensor_tensor(cmask[:], padf[:].rearrange("p (b k) -> p b k", b=NB),
                               mqk[:].unsqueeze(1).to_broadcast([P, NB, L]), ALU.add).then_inc(mask_ok, 1)
            separate_keys(0)
            separate_keys(1)
            separate_keys(2)
            inverse_deviation(1, TPH, TPH)
            pool.wait_ge(tg_ok, 1)
            pool.wait_ge(d_bo, 16)
            step(pool.tensor_tensor(bo_b[:], bo_b[:], tg[:, 0:1].to_broadcast([P, D]), ALU.mult))
            pool.wait_ge(d_x, 32)
            pool.tensor_tensor(xb_sb[:], x_sb[:], bo_b[:].unsqueeze(1).to_broadcast([P, NB, D]), ALU.add).then_inc(xb_ok, 1)

            def split_weights(t):
                s = t % WR
                pool.wait_ge(d_raw[s], raw_count[t])
                if t == 0:
                    pool.wait_ge(job_done, jn["kv", 1] + 1)
                gu = raw_gu[:, s]
                if t >= WR:
                    pool.wait_ge(u_done, LASTN[t - WR] + 1)
                step(pool.tensor_tensor(w_gu[0][:, s], gu, zero[:].unsqueeze(2).unsqueeze(3).to_broadcast([P, 2, DC, P]), ALU.add))
                pool.tensor_tensor(w_gu[1][:, s], gu, w_gu[0][:, s].bitcast(F32), ALU.subtract).then_inc(w_ok, 1)
                if t >= WR:
                    pool.wait_ge(y_done, 2 * (LASTN[t - WR] + 1))
                step(pool.tensor_tensor(w_d[0][:, s], raw_d[:, s], zero[:].to_broadcast([P, D]), ALU.add))
                pool.tensor_tensor(w_d[1][:, s], raw_d[:, s], w_d[0][:, s].bitcast(F32), ALU.subtract).then_inc(wd_ok, 1)

            for b in range(NB):
                if b + KZ < NB:
                    if b + KZ == TPH:
                        pool.wait_ge(*emptied(("kv", 1)))
                    separate_keys(b + KZ)
                if b == 1:
                    pool.memset(rw[0][:].bitcast(F32), 0.0)
                    pool.memset(rw[1][:].bitcast(F32), 0.0).then_inc(pool_init, 1)
                    pool.wait_ge(job_done, jn["q", 1, 1] + 1)
                    step(pool.memset(w_t[:, 0:FT * P + NT].bitcast(F32), 0.0))
                    pool.wait_ge(d_pick, 16)
                    pool.tensor_copy(pick_r[0:2 * E], pick_n[:]).then_inc(pick_ok, 1)
                if b in (3, 4, 5):
                    split_weights(b - 3)
                inverse_deviation(NQ + b, b, 1)
                if b in (TPH, NB - 1):
                    h = b // (NB - 1)
                    t4 = slice(h * TPH, (h + 1) * TPH)
                    pool.wait_ge(dif_ok, h + 1)
                    pool.tensor_tensor(e2[:, t4], cst[:, C_E:C_E + TPH], dif[:, t4], ALU.pow).then_inc(e2_ok, 1)
            for t in range(WR, FT):
                split_weights(t)

        @block.scalar
        def _(sc):
            sc.dma_start(cst[:], consts).then_inc(d_cst, 16)
            sc.dma_start(wkv_n[0:64, :], Wk).then_inc(d_wkv, 16)
            sc.dma_start(wkv_n[64:128, :], Wv).then_inc(d_wkv, 16)

            def high(j, parts=ALL):
                sc.wait_ge(job_done, jn[j] + 1)
                ps, k = jbank(j), j[0]
                if k == "wkv":
                    ins = nc.scalar.copy(wkv[0], ps[:, 0:NKW].rearrange("p (c n) -> p c n", c=DC))
                elif k == "wq":
                    for c in range(DC):
                        ins = nc.scalar.copy(wq[0][:, c].rearrange("p (r g d) -> p r g d", r=R, g=G),
                                             ps[:, c * D:(c + 1) * D].rearrange("p (g r d) -> p r g d", g=G, r=R))
                elif k == "wo":
                    ins = nc.scalar.copy(wo[0][:], ps[:].rearrange("p (c n) -> p c n", c=DC))
                elif k in ("c", "x"):
                    ins = nc.scalar.copy((cT if k == "c" else xT)[0][:, j[2], half(j[1])], ps[:])
                elif k == "kv":
                    if j[1] == 0:
                        sc.wait_ge(pool_init, 1)
                    for hf in range(2):
                        ins = nc.scalar.activation(k4[0:QR, hf, half(j[1])], ps[QR * hf:QR * (hf + 1), :],
                                                   ACT.Identity, bias=bias[QR * hf:QR * (hf + 1), 2 * R + hf:2 * R + hf + 1])
                        if hf == 0:
                            ins.then_inc(job_hi, 1)
                elif k == "q":
                    for i in parts:
                        hf, r, src = i % 2, 2 * j[2] + i // 2, QR * i
                        ins = nc.scalar.activation(q4[0:QR, hf, r, half(j[1])], ps[src:src + QR, :], ACT.Identity,
                                                   bias=bias[src:src + QR, hf * R + r:hf * R + r + 1])
                        if i != parts[-1]:
                            ins.then_inc(job_hi, 1)
                elif k == "MT":
                    rows = slice(3 * QR, KR)
                    src = ps[rows, :].rearrange("p (r q) -> p r q", r=R)
                    nc.scalar.copy(q4[rows, 0, :, toks(j[1])], src)
                    nc.scalar.copy(q4[rows, 1, :, toks(j[1])], src).then_inc(mt_ok, 1)
                    return
                elif k == "AT":
                    if j[1]:
                        sc.wait_ge(job_done, jn["WO", j[1] - 1] + 1)
                    ins = nc.scalar.copy(aT[0][:], ps[:, 0:D].rearrange("p (c q) -> p c q", c=DC))
                elif k == "YT":
                    ins = nc.scalar.copy(xT[0][:, :, toks(j[1])], ps[:, 0:D].rearrange("p (c q) -> p c q", c=DC))
                ins.then_inc(job_hi, 1)

            def take_values(h):
                nc.scalar.activation(vT[64:128, half(h)], jbank(("kv", h))[64:128, :], ACT.Identity,
                                     bias=bias[64:128, NBC - 1:NBC]).then_inc(v_ok, 1)

            for j in PHASE_A:
                if j == ("kv", 0):
                    sc.wait_ge(d_gate, 32)
                    nc.scalar.activation(tg[:], gate[:], ACT.Tanh).then_inc(tg_ok, 1)
                    sc.wait_ge(*emptied(("bias",)))
                if j in hn:
                    high(j)
                if j == ("q", 0, 1):
                    take_values(0)
            high(("MT", 0))

            def copy_o(b, hf):
                sc.wait_ge(pv_done, 2 * b + hf + 1)
                if b:
                    sc.wait_ge(job_done, jn["TO", b - 1, hf] + 1)
                nc.scalar.copy(o_sb[:, hf], bank[4 + hf][:]).then_inc(o_ok, 1)

            def silu(n):
                sc.wait_ge(g_done, n + 1)
                if n >= 2:
                    sc.wait_ge(u_free, n - 1)
                nc.scalar.activation(act_g[:, n % 2], bank[0][:], ACT.Silu).then_inc(a_ok, 1)

            for s in range(SLOTS):
                for j, parts in takes_at(s):
                    if j in hn or j[0] == "MT":
                        high(j, parts)
                    if j == ("kv", 1):
                        take_values(1)
                if s < CH:
                    b, i = s // G, s % G
                    sc.wait_ge(st_done, s + 1)
                    if b and i % 4 == 0:
                        sc.wait_ge(pv_done, 2 * (b - 1) + i // 4 + 1)
                    nc.scalar.activation(pT[:, i // 4, i % 4, :], bank[2 + s % 2][:], ACT.Exp,
                                         scale=SCALE).then_inc(p_done, 1)
                if s % G == 6 and s < CH:
                    copy_o(s // G, 0)
                if s % G == 1 and G < s < CH + G:
                    copy_o(s // G - 1, 1)
                for n, at in UP_SLOT.items():
                    if s == at + 1:
                        silu(n)
            for n in range(len(UP_SLOT), len(ORDER)):
                silu(n)

        @block.vector
        def _(ve):
            n_own = [0]

            def own(ins):
                n_own[0] += 1
                return ins.then_inc(vec, 1)

            def settle():
                ve.wait_ge(vec, n_own[0])

            def statistics(t0, n):
                for t in range(t0, t0 + n):
                    own(nc.vector.bn_stats(stats[:, t], x_sb[:, t]))
                settle()
                for t in range(t0, t0 + n):
                    ins = nc.vector.bn_aggr(mv[:, t], stats[:, t])
                ins.then_inc(var_ok, 1)

            def normalise(k, t0, n):
                ve.wait_ge(rstd_ok, k + 1)
                for t in range(t0, t0 + n):
                    ins = nc.vector.tensor_scalar(xn[:, t], x_sb[:, t], mv[:, t, 0:1], rstd[:, t:t + 1],
                                                  ALU.subtract, ALU.mult)
                ins.then_inc(xn_ok, 1)

            def minus(dst, ps, hi):
                return nc.vector.tensor_tensor(dst, ps, hi.bitcast(F32), ALU.subtract)

            def minus_biased(dst, ps, col, hi):
                return nc.vector.scalar_tensor_tensor(dst, ps, col, hi.bitcast(F32), ALU.add, ALU.subtract)

            def take(j, parts=ALL):
                ps, k = jbank(j), j[0]
                ve.wait_ge(job_done, jn[j] + 1)
                if j in hn and k not in ("q", "kv"):
                    ve.wait_ge(job_hi, hn[j] + 1)
                if k == "bias":
                    ins = nc.vector.tensor_copy(bias[:, 0:NBC], ps[:, 0:NBC])
                elif k == "wkv":
                    ins = minus(wkv[1], ps[:, 0:NKW].rearrange("p (c n) -> p c n", c=DC), wkv[0])
                elif k == "wq":
                    for c in range(DC):
                        ins = minus(wq[1][:, c].rearrange("p (r g d) -> p r g d", r=R, g=G),
                                    ps[:, c * D:(c + 1) * D].rearrange("p (g r d) -> p r g d", g=G, r=R),
                                    wq[0][:, c].rearrange("p (r g d) -> p r g d", r=R, g=G))
                elif k == "wo":
                    ins = minus(wo[1][:], ps[:].rearrange("p (c n) -> p c n", c=DC), wo[0][:])
                elif k in ("c", "x"):
                    t = cT if k == "c" else xT
                    ins = minus(t[1][:, j[2], half(j[1])], ps[:], t[0][:, j[2], half(j[1])])
                elif k == "kv":
                    s = half(j[1])
                    for hf in range(2):
                        ve.wait_ge(job_hi, hn[j] + hf + 1)
                        nc.vector.tensor_copy(k4[QR:2 * QR, hf, s], k4[0:QR, hf, s].bitcast(F32))
                        minus_biased(k4[2 * QR:3 * QR, hf, s], ps[QR * hf:QR * (hf + 1), :],
                                     bias[0:QR, 2 * R + hf:2 * R + hf + 1], k4[0:QR, hf, s]).then_inc(k_ok, 1)
                    return
                elif k == "vn":
                    ve.wait_ge(pool_init, 3)
                    ins = nc.vector.tensor_copy(vz[:, j[1] * TPH:(j[1] + 1) * TPH, :, 0:HD],
                                                ps[:, 0:TPH * 64].rearrange("p (b g d) -> p b g d", b=TPH, g=G))
                elif k == "q":
                    for i in parts:
                        ve.wait_ge(job_hi, hn[j] + i + 1)
                        hf, r, src = i % 2, 2 * j[2] + i // 2, QR * i
                        ins = minus_biased(q4[QR:2 * QR, hf, r, half(j[1])], ps[src:src + QR, :],
                                           bias[0:QR, hf * R + r:hf * R + r + 1], q4[0:QR, hf, r, half(j[1])])
                        if hf:
                            ins.then_inc(q_lo, 1)
                    return
                elif k == "TO":
                    _, b, hf = j
                    v = ps[:].rearrange("p (r j c) -> p r j c", r=R, c=VW)
                    if b:
                        ve.wait_ge(*emptied(("TO", b - 1, hf)))
                        ve.wait_ge(job_done, jn["AT", b - 1] + 1)
                    own(nc.vector.reciprocal(rden[:, hf], v[:, :, :, HD]))
                    settle()
                    a = an[:, 4 * hf:4 * hf + 4].rearrange("p j r d -> p r j d")
                    ins = nc.vector.tensor_tensor(a, v[:, :, :, 0:HD], rden[:, hf].unsqueeze(3).to_broadcast([P, R, 4, HD]),
                                                  ALU.mult)
                elif k == "AT":
                    ins = minus(aT[1][:], ps[:, 0:D].rearrange("p (c q) -> p c q", c=DC), aT[0][:])
                elif k == "WO":
                    b = j[1]
                    if b == 0:
                        ve.wait_ge(xb_ok, 1)
                    ins = nc.vector.scalar_tensor_tensor(x_sb[:, b], ps[:, 0:D], tg[:, 0:1], xb_sb[:, b], ALU.mult, ALU.add)
                elif k == "YT":
                    s = toks(j[1])
                    ins = minus(xT[1][:, :, s], ps[:, 0:D].rearrange("p (c q) -> p c q", c=DC), xT[0][:, :, s])
                elif k == "SC":
                    ins = nc.vector.tensor_copy(s16[0:E, half(j[1])], ps[0:E, :])
                elif k == "SN":
                    t = slice(j[1] * TPH, (j[1] + 1) * TPH)
                    ins = nc.vector.tensor_copy(sn[:, t], ps[:, 0:TPH * E].rearrange("p (b e) -> p b e", b=TPH))
                elif k == "CT":
                    ins = nc.vector.tensor_copy(cwT[0:2 * E, half(j[1])], ps[0:2 * E, :])
                ins.then_inc(job_lo, 1)
                if k == "WO":
                    ve.wait_ge(*emptied(j))
                    statistics(j[1], 1)

            ve.wait_ge(d_x0, 16)
            for t in range(TPH):
                if t == 2:
                    ve.wait_ge(d_x, 16)
                own(nc.vector.bn_stats(stats[:, t], x_sb[:, t]))
            settle()
            for t in range(TPH):
                ins = nc.vector.bn_aggr(mv[:, t], stats[:, t])
            ins.then_inc(var_ok, 1)
            take(("wkv",))
            normalise(0, 0, TPH)
            take(("c", 0, 0))
            take(("c", 0, 1))
            take(("wq",))
            ve.wait_ge(d_b, 64)
            nc.vector.tensor_copy(bperm[0:2 * R + 2, QR:P].rearrange("p (u n) -> p u n", n=QR),
                                  bperm[0:2 * R + 2, 0:QR].unsqueeze(1).to_broadcast([2 * R + 2, P // QR - 1, QR])).then_inc(brow_ok, 1)
            take(("x", 0, 0))
            take(("x", 0, 1))
            ve.wait_ge(d_mask, 32)
            nc.vector.tensor_scalar(mqk[:], mqk_u[:], -BIG, None, ALU.mult).then_inc(masks_f, 1)
            nc.vector.tensor_scalar(padf[:], pad_u[:], -BIG, None, ALU.mult).then_inc(masks_f, 1)
            take(("bias",))
            take(("kv", 0))
            take(("q", 0, 0))

            def row_max(n):
                r, hf = n % G // 2, n % 2
                ve.wait_ge(s_done, n + 1)
                if n >= G:
                    ve.wait_ge(m_parts, n // G)
                nc.vector.tensor_reduce(mneg[:, r, 4 * hf:4 * hf + 4], bank[n % 2][:].rearrange("p (g k) -> p g k", g=4),
                                        X, ALU.max, negate=True).then_inc(max_ok, 1)

            def max_parts(b):
                ve.wait_ge(max_ok, G * (b + 1))
                if b:
                    ve.wait_ge(job_done, jn["MT", b - 1] + 1)
                else:
                    ve.wait_ge(pool_init, 3)
                own(nc.vector.tensor_copy(mt[:, :, 3 * QR:3 * QR + G], mneg[:]))
                settle()
                nc.vector.tensor_tensor(mt[:, :, 3 * QR + G:KR], mneg[:], mt[:, :, 3 * QR:3 * QR + G].bitcast(F32), ALU.subtract).then_inc(m_parts, 1)

            def best_two(h):
                ve.wait_ge(*emptied(("SN", h)))
                tiles = range(h * TPH, (h + 1) * TPH)
                t4 = slice(h * TPH, (h + 1) * TPH)
                for t in tiles:
                    own(nc.vector.max(top[:, t], sn[:, t]))
                settle()
                nc.vector.tensor_tensor(dif[:, t4], top[:, t4, 1], top[:, t4, 0], ALU.subtract).then_inc(dif_ok, 1)
                for t in tiles:
                    own(nc.vector.max_index(topi[:, t], top[:, t], sn[:, t]))
                settle()
                own(nc.vector.tensor_copy(topf[:, t4, 0:2], topi[:, t4, 0:2]))
                settle()
                iota = cst[:, C_IOTA:C_IOTA + E].unsqueeze(1).to_broadcast([P, TPH, E])
                for i, cb in enumerate((cb1, cb2)):
                    own(nc.vector.tensor_tensor(cb[:, t4], iota, topf[:, t4, i].unsqueeze(2).to_broadcast([P, TPH, E]),
                                                ALU.is_equal))

            def expert_weights(h):
                t4 = slice(h * TPH, (h + 1) * TPH)
                ve.wait_ge(e2_ok, h + 1)
                own(nc.vector.tensor_scalar(den2[:, t4], e2[:, t4], 1.0, None, ALU.add))
                settle()
                own(nc.vector.reciprocal(inv2[:, t4], den2[:, t4]))
                settle()
                own(nc.vector.tensor_scalar(w1[:, t4], inv2[:, t4], tg[:, 1:2], None, ALU.mult))
                own(nc.vector.scalar_tensor_tensor(w2[:, t4], inv2[:, t4], tg[:, 1:2], e2[:, t4], ALU.mult, ALU.mult))
                settle()
                for cb, w in ((cb1, w1), (cb2, w2)):
                    own(nc.vector.tensor_tensor(cb[:, t4], cb[:, t4], w[:, t4].unsqueeze(2).to_broadcast([P, TPH, E]),
                                                ALU.mult))
                settle()
                own(nc.vector.tensor_tensor(comb[:, t4], cb1[:, t4], cb2[:, t4], ALU.add))
                own(nc.vector.tensor_tensor(c2[:, t4, 0], cb1[:, t4], cb2[:, t4], ALU.add))
                settle()
                nc.vector.tensor_tensor(c2[:, t4, 1], comb[:, t4], c2[:, t4, 0].bitcast(F32), ALU.subtract).then_inc(c2_ok, 1)

            def gated(n):
                ve.wait_ge(a_ok, n + 1)
                ve.wait_ge(u_done, n + 1)
                if n == 0:
                    ve.wait_ge(pv_done, 2 * NB)
                if n >= UL:
                    ve.wait_ge(job_lo, ln["CB", n - UL] + 1)
                nc.vector.tensor_tensor(h_su[:, n % UL], act_g[:, n % 2], bank[1][:], ALU.mult).then_inc(u_free, 1)

            def weigh(n):
                j = ("CB", n)
                ve.wait_ge(u_free, n + 1)
                ve.wait_ge(job_done, jn[j] + 1)
                if n:
                    ve.wait_ge(h_ok, n)
                nc.vector.tensor_tensor(h_all, h_su[:, n % UL], jbank(j)[:], ALU.mult).then_inc(job_lo, 1)
                ve.wait_ge(*emptied(j))
                if n >= 2:
                    ve.wait_ge(y_done, 2 * (n - 1))
                own(nc.vector.tensor_copy(hh[:, n % 2], h_all))
                settle()
                nc.vector.tensor_tensor(hl[:, n % 2], h_all, hh[:, n % 2].bitcast(F32), ALU.subtract).then_inc(h_ok, 1)

            take(("q", 0, 1), (0, 1))
            for n in range(G):
                row_max(n)
                if n == 1:
                    take(("q", 0, 1), (2, 3))
            max_parts(0)
            for n in range(G, LEAD):
                row_max(n)
            take(("c", 1, 0))
            take(("c", 1, 1))
            ve.wait_ge(d_x, 32)
            for s in range(SLOTS):
                if s == 0:
                    statistics(TPH, TPH)
                if s == 20:
                    ve.wait_ge(pool_init, 4)
                    ve.wait_ge(d_rw, 16)
                    own(nc.vector.tensor_copy(rw[0][:, :, 0:E], rw_n[:]))
                    settle()
                    nc.vector.tensor_tensor(rw[1][:, :, 0:E], rw_n[:], rw[0][:, :, 0:E].bitcast(F32), ALU.subtract).then_inc(rw_ok, 1)
                for j, parts in takes_at(s):
                    if j[0] == "CB":
                        weigh(j[1])
                    elif j[0] != "MT":
                        take(j, parts)
                for n in ahead(s):
                    row_max(n)
                    if n % G == G - 1:
                        max_parts(n // G)
                if s == 2:
                    normalise(1, TPH, TPH)
                for b in range(NB):
                    if s == NORM_SLOT[b]:
                        normalise(NQ + b, b, 1)
                for h in range(NQ):
                    if s == ROUTE["best"][h]:
                        best_two(h)
                    if s == ROUTE["weights"][h]:
                        expert_weights(h)
                for n, at in UP_SLOT.items():
                    if s == at + 1:
                        gated(n)
            for n in range(len(DOWN_SLOT), len(ORDER)):
                if n + 1 < len(ORDER):
                    weigh(n + 1)
                if n + UL < len(ORDER):
                    gated(n + UL)
            for y in range(NB // 2):
                ve.wait_ge(y_done, 2 * (len(ORDER) - NQ + y // 2) + y % 2 + 1)
                for t in (2 * y, 2 * y + 1):
                    ins = nc.vector.tensor_tensor(x_sb[:, t], bank[2 + y][:, t % 2 * D:(t % 2 + 1) * D], x_sb[:, t], ALU.add)
                ins.then_inc(fin_ok, 1)

        @block.tensor
        def _(pe):
            def mm(dst, a, b, start, stop):
                return nc.tensor.matmul(dst, a, b, start=start, stop=stop, skip_group_check=True)

            def three(dst, st, mv_, chunks, first=True):
                terms = [(st[0], mv_[0]), (st[0], mv_[1]), (st[1], mv_[0])]
                last = None
                for c in range(chunks):
                    for k, (a, b) in enumerate(terms):
                        last = mm(dst, a(c), b(c), first and c == 0 and k == 0, c == chunks - 1 and k == 2)
                return last

            def job(j):
                if before(j) is not None:
                    pe.wait_ge(*emptied(before(j)))
                    if before(j)[0] == "kv":
                        pe.wait_ge(v_ok, before(j)[1] + 1)
                ps, k = jbank(j), j[0]
                if k == "bias":
                    pe.wait_ge(brow_ok, 1)
                    pe.wait_ge(d_cst, 16)
                    ins = nc.tensor.transpose(ps[:, 0:NBC], bperm[:], ident[0:NBC, 0:NBC])
                elif k == "wkv":
                    pe.wait_ge(d_wkv, 32)
                    for c in range(DC):
                        ins = nc.tensor.transpose(ps[:, c * P:(c + 1) * P], wkv_n[:, c * P:(c + 1) * P], ident)
                elif k in ("wq", "wo"):
                    src = wq_n if k == "wq" else wo_n
                    pe.wait_ge(d_wq if k == "wq" else d_wo, 16)
                    for c in range(DC):
                        for o in range(DC):
                            ins = nc.tensor.transpose(ps[:, c * D + o * P:c * D + (o + 1) * P],
                                                      src[:, o, c * P:(c + 1) * P], ident)
                elif k in ("c", "x"):
                    _, h, c = j
                    if k == "c":
                        pe.wait_ge(d_ctx, 16 * (h + 1))
                    else:
                        pe.wait_ge(xn_ok, h + 1)
                    src = c_sb if k == "c" else xn
                    for t in range(TPH):
                        ins = nc.tensor.transpose(ps[:, toks(t)], src[:, h * TPH + t, c * P:(c + 1) * P], ident)
                elif k == "vn":
                    pe.wait_ge(v_ok, j[1] + 1)
                    for b in range(TPH):
                        ins = nc.tensor.transpose(ps[:, b * 64:(b + 1) * 64], vT[64:128, toks(j[1] * TPH + b)],
                                                  ident[64:128, 64:128])
                elif k == "kv":
                    pe.wait_ge(*emptied(("c", j[1], 1)))
                    ins = three(ps[:], [lambda c, i=i: wkv[i][:, c] for i in range(2)],
                                [lambda c, i=i: cT[i][:, c, half(j[1])] for i in range(2)], DC)
                elif k == "q":
                    pe.wait_ge(*emptied(("x", j[1], 1)))
                    ins = three(ps[:], [lambda c, i=i: wq[i][:, c, j[2] * P:(j[2] + 1) * P] for i in range(2)],
                                [lambda c, i=i: xT[i][:, c, half(j[1])] for i in range(2)], DC)
                elif k == "MT":
                    pe.wait_ge(m_parts, j[1] + 1)
                    for r in range(R):
                        ins = nc.tensor.transpose(ps[0:KR, r * L:(r + 1) * L], mt[:, r].bitcast(F32), ident)
                elif k == "TO":
                    pe.wait_ge(o_ok, 2 * j[1] + j[2] + 1)
                    for r in range(R):
                        ins = nc.tensor.transpose(ps[:, r * P:(r + 1) * P], o_sb[:, j[2], r * L:(r + 1) * L], ident)
                elif k == "AT":
                    pe.wait_ge(*emptied(("TO", j[1], 1)))
                    a = an[:].rearrange("p g r d -> p (g r d)")
                    for c in range(DC):
                        ins = nc.tensor.transpose(ps[:, c * L:(c + 1) * L], a[:, c * P:(c + 1) * P], ident)
                elif k == "WO":
                    pe.wait_ge(*emptied(("AT", j[1])))
                    ins = three(ps[:, 0:D], [lambda c, i=i: aT[i][:, c] for i in range(2)],
                                [lambda c, i=i: wo[i][:, c] for i in range(2)], DC)
                elif k == "YT":
                    pe.wait_ge(xn_ok, NQ + j[1] + 1)
                    for c in range(DC):
                        ins = nc.tensor.transpose(ps[:, c * L:(c + 1) * L], xn[:, j[1], c * P:(c + 1) * P], ident)
                elif k == "SC":
                    pe.wait_ge(*emptied(("YT", (j[1] + 1) * TPH - 1)))
                    pe.wait_ge(rw_ok, 1)
                    ins = three(ps[:], [lambda c, i=i: rw[i][:, c] for i in range(2)],
                                [lambda c, i=i: xT[i][:, c, half(j[1])] for i in range(2)], DC)
                elif k == "SN":
                    pe.wait_ge(*emptied(("SC", j[1])))
                    for t in range(TPH):
                        ins = nc.tensor.transpose(ps[:, t * E:(t + 1) * E], s16[0:E, toks(j[1] * TPH + t)], ident[0:E, 0:E])
                elif k == "CT":
                    pe.wait_ge(c2_ok, j[1] + 1)
                    for t in range(TPH):
                        ins = nc.tensor.transpose(ps[0:2 * E, toks(t)],
                                                  c2[:, j[1] * TPH + t].rearrange("p a e -> p (a e)").bitcast(F32), ident)
                elif k == "CB":
                    t, h = ORDER[j[1]]
                    pe.wait_ge(*emptied(("CT", h)))
                    pe.wait_ge(pick_ok, 1)
                    ins = mm(ps[:], pick_r[:, t * P:(t + 1) * P], cwT[:, half(h)], True, True)
                ins.then_inc(job_done, 1)

            for j in PHASE_A[:NA - 1]:
                job(j)

            def scores_q(n):
                b, r, hf = n // G, n % G // 2, n % 2
                if n >= 2:
                    pe.wait_ge(max_ok, n - 1)
                if n % G < 2:
                    pe.wait_ge(kz_ok, 2 * b + hf + 1)
                if b % TPH == 0 and hf == 0:
                    pe.wait_ge(q_lo, R * (b // TPH) + r + 1)
                    pe.wait_ge(d_q4[b // TPH][r], 16)
                s, g4, ps = b % KZ, slice(4 * hf, 4 * hf + 4), bank[n % 2]
                mm(ps[:], q4[0:3 * QR, hf, r, toks(b)], kz[0:3 * QR, s, g4].rearrange("p g k -> p (g k)"), True, False)
                mm(ps[:], ident_b[:], cmask[:, b].unsqueeze(1).to_broadcast([P, 4, L]), False, True).then_inc(s_done, 1)

            def scores_k(n):
                b, g = n // G, n % G
                if n >= 2:
                    pe.wait_ge(p_done, n - 1)
                if g == 0:
                    pe.wait_ge(*emptied(("MT", b)))
                s, ps = b % KZ, bank[2 + n % 2][:].rearrange("p (r q) -> p r q", r=R)
                mm(ps, cmask[:, b], ident_b[:].unsqueeze(1).to_broadcast([P, R, L]), True, False)
                mm(ps, kz[0:KR, s, g], q4[0:KR, g // GH, :, toks(b)], False, True).then_inc(st_done, 1)

            def weigh_values(b, hf):
                pe.wait_ge(p_done, G * b + 4 * hf + 4)
                if b:
                    pe.wait_ge(o_ok, 2 * (b - 1) + hf + 1)
                for j in range(4):
                    ins = mm(bank[4 + hf][VW * j:VW * (j + 1), :], vz[:, b, 4 * hf + j], pT[:, hf, j], True, True)
                ins.then_inc(pv_done, 1)

            def up(n):
                t, h = ORDER[n]
                s = t % WR
                pe.wait_ge(w_ok, t + 1)
                pe.wait_ge(*emptied(("YT", (h + 1) * TPH - 1)))
                if n == 0:
                    pe.wait_ge(max_ok, CH)
                for m, done, free in ((0, g_done, a_ok), (1, u_done, u_free)):
                    if n:
                        pe.wait_ge(free, n)
                    three(bank[m][:], [lambda c, i=i: w_gu[i][:, s, m, c] for i in range(2)],
                          [lambda c, i=i: xT[i][:, c, half(h)] for i in range(2)], DC).then_inc(done, 1)

            def down(n):
                t, h = ORDER[n]
                s = t % WR
                pe.wait_ge(wd_ok, t + 1)
                pe.wait_ge(h_ok, n + 1)
                if n == 0:
                    pe.wait_ge(p_done, CH)
                    pe.wait_ge(o_ok, 2 * NB)
                for u in range(TPH):
                    ins = three(bank[2 + (h * TPH + u) // 2][:, u % 2 * D:(u % 2 + 1) * D],
                                [lambda c, i=i: (hh, hl)[i][:, n % 2, toks(u)] for i in range(2)],
                                [lambda c, i=i: w_d[i][:, s] for i in range(2)], 1, first=(t == 0 and u % 2 == 0))
                    if u % 2:
                        ins.then_inc(y_done, 1)

            pe.wait_ge(mask_ok, 1)
            pe.wait_ge(pool_init, 3)
            for n in range(LEAD):
                scores_q(n)
            job(("MT", 0))
            for s in range(SLOTS):
                if s < CH:
                    scores_k(s)
                for n in ahead(s):
                    scores_q(n)
                if s % G == 5 and s < CH:
                    weigh_values(s // G, 0)
                if s % G == 0 and 0 < s <= CH:
                    weigh_values(s // G - 1, 1)
                for j in jobs_at(s):
                    job(j)
                for n, at in UP_SLOT.items():
                    if s == at:
                        up(n)
                for n, at in DOWN_SLOT.items():
                    if s == at:
                        down(n)
            for n in range(len(DOWN_SLOT), len(ORDER)):
                if n + 1 < len(ORDER) and n + 1 not in CB_SLOT:
                    job(("CB", n + 1))
                if n + UL < len(ORDER):
                    up(n + UL)
                down(n)


_INS = ['x', 'ctx_2048', 'mask_SxS2_bc0', 'mask_BxS2_bk0', 'g_xattn', 'g_ffn', 'L0_xattn_Wq', 'L0_xattn_bq',
        'L0_xattn_Wk', 'L0_xattn_bk', 'L0_xattn_Wv', 'L0_xattn_bv', 'L0_xattn_Wo', 'L0_xattn_bo',
        'L0_ffn_router_w', 'L0_ffn_gate_w', 'L0_ffn_up_w', 'L0_ffn_down_w']


def kernel(**inputs):
    import concourse.bacc as _bacc
    from concourse.bass_utils import run_bass_kernel_spmd as _run

    nc = _bacc.Bacc("TRN2", target_bir_lowering=False, num_devices=1)
    arrays, args = {}, []
    for name in _INS:
        a = np.ascontiguousarray(inputs[name])
        arrays[f"in_{name}"] = a
        args.append(nc.dram_tensor(f"in_{name}", a.shape, mybir.dt.from_np(a.dtype), kind="ExternalInput").ap())
    c = shape_constants()
    arrays["shape_constants"] = c
    args.append(nc.dram_tensor("shape_constants", c.shape, F32, kind="ExternalInput").ap())
    c = expert_rows()
    arrays["expert_rows"] = c
    args.append(nc.dram_tensor("expert_rows", c.shape, U8, kind="ExternalInput").ap())
    args.append(nc.dram_tensor("out_0", (NB, L, D), F32, kind="ExternalOutput").ap())
    build(nc, *args)
    r = _run(nc, [arrays], core_ids=[0])
    return r.results[0]["out_0"]
```
